# Optimizing a Trainium2 kernel written in Bass

```python
import numpy as np
import jax
import jax.numpy as jnp

def _softmax(x, axis=-1):
    return jax.nn.softmax(x, axis=axis)

def _gelu(x):
    return jax.nn.gelu(x, approximate=True)

def _silu(x):
    return jax.nn.silu(x)

def _sigmoid(x):
    return jax.nn.sigmoid(x)

def _layernorm(x, axis=-1, eps=1e-05):
    m = jnp.mean(x, axis=axis, keepdims=True)
    v = jnp.var(x, axis=axis, keepdims=True)
    return (x - m) / jnp.sqrt(v + eps)

def _scatter_add(tgt, idx, src, axis=0):
    return tgt.at[idx].add(src)

def _segment_sum(src, seg, n):
    return jax.ops.segment_sum(src, seg, n)
kernel_name = 'mk_audio_tower_d1_tok_audfeat768_r4_da238d'

def setup_inputs(seed: int=0):
    np.random.seed(seed)
    _w = jnp.asarray

    def _rec_inputs():
        import jax
        import jax.numpy as jnp
        _rk = jax.random.key(seed)
        x = -4.65018e-05 + 0.999886 * jax.random.normal(jax.random.fold_in(_rk, 1), (64, 256, 192), jnp.float32)
        return x
    x = _rec_inputs()

    def _L0_tok_setup():
        import jax, jax.numpy as jnp
        import numpy as np
        key = jax.random.key(seed)
        ks = jax.random.split(key, 8)
        B, S, TD, DM = (16, 1024, 192, 192)
        s = 0.02
        return {'text_embeddings': jax.random.normal(ks[0], (B, S, TD), jnp.float32), 'W_w': jax.random.normal(ks[1], (DM, TD), jnp.float32) * s, 'W_b': jax.random.normal(ks[2], (DM,), jnp.float32) * s, 'b': jnp.zeros((DM,), jnp.float32), 'V_w': jax.random.normal(ks[3], (1, DM), jnp.float32) * s, 'V_b': jax.random.normal(ks[4], (1,), jnp.float32) * s, 'P_w': jax.random.normal(ks[5], (DM, TD), jnp.float32) * s, 'P_b': jax.random.normal(ks[6], (DM,), jnp.float32) * s, 'patch_len': 4, 'stride': 2}
    _L0_tok_all = _L0_tok_setup()
    _L0_tok_in = {k: v for k, v in _L0_tok_all.items() if k in ('W_w', 'W_b', 'b', 'V_w', 'V_b', 'P_w', 'P_b')}
    del _L0_tok_all

    def _L0_attn_setup():
        import jax, jax.numpy as jnp
        import numpy as np
        import math
        LATENT_RANK = 64
        NUM_HEADS = 12
        HEAD_DIM = 64
        key = jax.random.key(seed)
        k1, k2, k3, k4, k5 = jax.random.split(key, 5)
        b, n, h = (8, 256, 192)
        r, nh = (LATENT_RANK, NUM_HEADS)
        std = 0.02
        return {'hidden_states': jax.random.normal(k1, (b, n, h), dtype=jnp.float32), 'basis_w': jax.random.normal(k2, (r, h), dtype=jnp.float32) * std, 'core': jax.random.normal(k3, (r, r), dtype=jnp.float32) * std, 'head_residual': jax.random.normal(k4, (nh, r, r), dtype=jnp.float32) * (std / 10.0), 'value_w': jax.random.normal(k5, (h, h), dtype=jnp.float32) * std, 'value_b': jnp.zeros((h,), dtype=jnp.float32)}
    _L0_attn_all = _L0_attn_setup()
    _L0_attn_in = {k: v for k, v in _L0_attn_all.items() if k in ('basis_w', 'core', 'head_residual', 'value_w', 'value_b')}
    del _L0_attn_all

    def _L0_ffn_setup():
        import jax, jax.numpy as jnp
        import numpy as np
        from jax import lax
        DIM = 192
        INTER = 128
        E = 8
        G = 4
        TOPK_G = 2
        TOPK = 2
        ROUTE_SCALE = 1.0

        def _gate(x2, gate_weight, gate_bias):
            T = x2.shape[0]
            scores = jax.nn.sigmoid(x2 @ gate_weight.T)
            s = scores + gate_bias
            sv = s.reshape(T, G, E // G)
            top2, _ = lax.top_k(sv, 2)
            group_scores = top2.sum(-1)
            _, gidx = lax.top_k(group_scores, TOPK_G)
            gmask = jnp.zeros((T, G), bool).at[jnp.arange(T)[:, None], gidx].set(True)
            masked = jnp.where(gmask[:, :, None], sv, -jnp.inf).reshape(T, E)
            _, idx = lax.top_k(masked, TOPK)
            w = jnp.take_along_axis(scores, idx, axis=1)
            w = w / (w.sum(-1, keepdims=True) + 1e-06) * ROUTE_SCALE
            return (w, idx)
        key = jax.random.key(seed)
        ks = jax.random.split(key, 9)
        s = 1.0 / np.sqrt(DIM)
        si = 1.0 / np.sqrt(INTER)
        return {'x': jax.random.normal(ks[0], (4, 1024, DIM), jnp.float32), 'gate_weight': jax.random.uniform(ks[1], (E, DIM), jnp.float32, -s, s), 'gate_bias': jnp.zeros((E,), jnp.float32), 'w1': jax.random.uniform(ks[2], (E, INTER, DIM), jnp.float32, -s, s), 'w2': jax.random.uniform(ks[3], (E, DIM, INTER), jnp.float32, -si, si), 'w3': jax.random.uniform(ks[4], (E, INTER, DIM), jnp.float32, -s, s), 'sw1': jax.random.uniform(ks[5], (INTER, DIM), jnp.float32, -s, s), 'sw2': jax.random.uniform(ks[6], (DIM, INTER), jnp.float32, -si, si), 'sw3': jax.random.uniform(ks[7], (INTER, DIM), jnp.float32, -s, s)}
    _L0_ffn_all = _L0_ffn_setup()
    _L0_ffn_in = {k: v for k, v in _L0_ffn_all.items() if k in ('gate_weight', 'gate_bias', 'w1', 'w2', 'w3', 'sw1', 'sw2', 'sw3')}
    del _L0_ffn_all
    return {'x': x, 'L0_tok_W_w': _L0_tok_in['W_w'], 'L0_tok_W_b': _L0_tok_in['W_b'], 'L0_tok_b': _L0_tok_in['b'], 'L0_tok_V_w': _L0_tok_in['V_w'], 'L0_tok_V_b': _L0_tok_in['V_b'], 'L0_tok_P_w': _L0_tok_in['P_w'], 'L0_tok_P_b': _L0_tok_in['P_b'], 'L0_attn_basis_w': _L0_attn_in['basis_w'], 'L0_attn_core': _L0_attn_in['core'], 'L0_attn_head_residual': _L0_attn_in['head_residual'], 'L0_attn_value_w': _L0_attn_in['value_w'], 'L0_attn_value_b': _L0_attn_in['value_b'], 'L0_ffn_gate_weight': _L0_ffn_in['gate_weight'], 'L0_ffn_gate_bias': _L0_ffn_in['gate_bias'], 'L0_ffn_w1': _L0_ffn_in['w1'], 'L0_ffn_w2': _L0_ffn_in['w2'], 'L0_ffn_w3': _L0_ffn_in['w3'], 'L0_ffn_sw1': _L0_ffn_in['sw1'], 'L0_ffn_sw2': _L0_ffn_in['sw2'], 'L0_ffn_sw3': _L0_ffn_in['sw3']}

def reference(x, L0_tok_W_w, L0_tok_W_b, L0_tok_b, L0_tok_V_w, L0_tok_V_b, L0_tok_P_w, L0_tok_P_b, L0_attn_basis_w, L0_attn_core, L0_attn_head_residual, L0_attn_value_w, L0_attn_value_b, L0_ffn_gate_weight, L0_ffn_gate_bias, L0_ffn_w1, L0_ffn_w2, L0_ffn_w3, L0_ffn_sw1, L0_ffn_sw2, L0_ffn_sw3):
    import jax
    import jax.numpy as jnp

    def _L0_tok_ref(text_embeddings, W_w, W_b, b, V_w, V_b, P_w, P_b, patch_len, stride):
        import jax, jax.numpy as jnp
        import numpy as np
        B, S, TD = text_embeddings.shape
        A = jnp.tanh(jnp.einsum('bst,dt->bsd', text_embeddings, W_w) + W_b + b)
        scores = jnp.einsum('bsd,od->bso', A, V_w)[..., 0] + V_b[0]
        starts = jnp.arange(0, S - patch_len + 1, stride)
        idx = starts[:, None] + jnp.arange(patch_len)
        sw = scores[:, idx]
        w = jax.nn.softmax(sw, axis=-1)
        xw = text_embeddings[:, idx]
        attended = jnp.einsum('bpl,bplt->bpt', w, xw)
        return jnp.einsum('bpt,dt->bpd', attended, P_w) + P_b

    def _L0_attn_ref(hidden_states, basis_w, core, head_residual, value_w, value_b):
        import jax, jax.numpy as jnp
        import numpy as np
        import math
        LATENT_RANK = 64
        NUM_HEADS = 12
        HEAD_DIM = 64
        b, n, hidden = hidden_states.shape
        nh, r = (head_residual.shape[0], core.shape[0])
        hd = hidden // nh
        latent = jnp.einsum('bnh,rh->bnr', hidden_states, basis_w)
        centered = head_residual - jnp.mean(head_residual, axis=0, keepdims=True)
        head_mats = core[None, :, :] / float(nh) + centered
        scores = jnp.einsum('bnr,hrs,bms->bhnm', latent, head_mats, latent)
        scores = scores / math.sqrt(float(r))
        probs = jax.nn.softmax(scores, axis=-1)
        v = jnp.einsum('bnh,oh->bno', hidden_states, value_w) + value_b
        v = v.reshape(b, n, nh, hd).transpose(0, 2, 1, 3)
        ctx = jnp.einsum('bhnm,bhmd->bhnd', probs, v)
        ctx = ctx.transpose(0, 2, 1, 3).reshape(b, n, hidden)
        return ctx

    def _L0_ffn_ref(x, gate_weight, gate_bias, w1, w2, w3, sw1, sw2, sw3):
        import jax, jax.numpy as jnp
        import numpy as np
        from jax import lax
        DIM = 192
        INTER = 128
        E = 8
        G = 4
        TOPK_G = 2
        TOPK = 2
        ROUTE_SCALE = 1.0

        def _gate(x2, gate_weight, gate_bias):
            T = x2.shape[0]
            scores = jax.nn.sigmoid(x2 @ gate_weight.T)
            s = scores + gate_bias
            sv = s.reshape(T, G, E // G)
            top2, _ = lax.top_k(sv, 2)
            group_scores = top2.sum(-1)
            _, gidx = lax.top_k(group_scores, TOPK_G)
            gmask = jnp.zeros((T, G), bool).at[jnp.arange(T)[:, None], gidx].set(True)
            masked = jnp.where(gmask[:, :, None], sv, -jnp.inf).reshape(T, E)
            _, idx = lax.top_k(masked, TOPK)
            w = jnp.take_along_axis(scores, idx, axis=1)
            w = w / (w.sum(-1, keepdims=True) + 1e-06) * ROUTE_SCALE
            return (w, idx)
        B, S, D = x.shape
        x2 = x.reshape(-1, D)
        T = x2.shape[0]
        weights, indices = _gate(x2, gate_weight, gate_bias)
        cw = jnp.zeros((T, E), x.dtype).at[jnp.arange(T)[:, None], indices].add(weights)
        h1 = jnp.einsum('td,eid->tei', x2, w1)
        h3 = jnp.einsum('td,eid->tei', x2, w3)
        h = jax.nn.silu(h1) * h3
        y = jnp.einsum('tei,edi,te->td', h, w2, cw)
        z = jax.nn.silu(x2 @ sw1.T) * (x2 @ sw3.T) @ sw2.T
        return (y + z).reshape(B, S, D)
    h = _L0_tok_ref(x, L0_tok_W_w, L0_tok_W_b, L0_tok_b, L0_tok_V_w, L0_tok_V_b, L0_tok_P_w, L0_tok_P_b, 4, 2)
    h = h + _L0_attn_ref(_layernorm(h, axis=-1), L0_attn_basis_w, L0_attn_core, L0_attn_head_residual, L0_attn_value_w, L0_attn_value_b)
    h = h + _L0_ffn_ref(_layernorm(h, axis=-1), L0_ffn_gate_weight, L0_ffn_gate_bias, L0_ffn_w1, L0_ffn_w2, L0_ffn_w3, L0_ffn_sw1, L0_ffn_sw2, L0_ffn_sw3)
    return h

_drawn_inputs = setup_inputs


def setup_inputs(seed=0):
    import zlib

    import numpy as np

    out = dict(_drawn_inputs(seed))
    spreads = {'L0_tok_b': (0.0, 0.517), 'L0_attn_value_b': (0.0, 0.1), 'L0_ffn_gate_bias': (0.0, 0.1)}
    factors = {'L0_tok_W_b': 22.205,
     'L0_attn_basis_w': 8.0,
     'L0_attn_core': 8.0,
     'L0_attn_head_residual': 8.0}
    for name, (base, spread) in spreads.items():
        noise = np.random.default_rng([zlib.crc32(name.encode()), seed]).standard_normal(out[name].shape)
        drawn = base * np.exp(spread * noise) if base else spread * noise
        out[name] = jnp.asarray(drawn.astype(out[name].dtype))
    for name, factor in factors.items():
        out[name] = (out[name] * factor).astype(out[name].dtype)
    return out
```

```python
import numpy as np
import concourse.bass as bass
from concourse import mybir
from contextlib import ExitStack

F32 = mybir.dt.float32
F16 = mybir.dt.float16
I32 = mybir.dt.int32
ALU = mybir.AluOpType
ACT = mybir.ActivationFunctionType
AX = mybir.AxisListType

B, S, D = 64, 256, 192
PL, STRIDE = 4, 2
P = (S - PL) // STRIDE + 1
NH, R = 12, 64
HD = D // NH
HV = HD + 1
U = 4
NU = NH // U
UW = U * P
E, TOPK, G = 8, 2, 4
I = 128
NE = E + 1
CUT = D + 1 - 128
SHIFT = 2.0 ** 15
TB = 4
NG = B // TB
LAST = B + 6
HEAD, TAIL = 8, B


def on(n):
    return not isinstance(n, int) or 0 <= n < B


def later(n, k):
    return not isinstance(n, int) or n >= k


def it_first(it, first):
    return isinstance(it, int) and it == first


def walk(eng, step):
    for it in range(HEAD):
        step(it, it % 2)
    with eng.Fori(HEAD // 2, TAIL // 2) as pair:
        for odd in range(2):
            step(2 * pair + odd, odd)
    for it in range(TAIL, LAST):
        step(it, it % 2)


def windows(x):
    return bass.AP(tensor=x.tensor, offset=0, ap=[[S * D, B], [STRIDE * D, P], [1, PL * D]])


def audio_tower(nc, x, w_tok, b_tok, v_tok, vb_tok, p_tok, attn_w, attn_vb, core, head_res,
                gate_w, gate_b, w1, w3, w2, eye, shift, out):
    with ExitStack() as ctx:
        def sb(name, shape, dt=F32):
            return ctx.enter_context(nc.sbuf_tensor(name, shape, dt))

        def bank(name, n=1):
            return ctx.enter_context(nc.psum_tensor(name, [128, n * 512], F32))

        def sem(name):
            return ctx.enter_context(nc.semaphore(name))

        w_tok_s = sb("w_tok_s", [128, 2, D])
        b_tok_s = sb("b_tok_s", [128, D])
        v_tok_s = sb("v_tok_s", [128, D])
        vb_s = sb("vb_s", [128, 1])
        p_tok_s = sb("p_tok_s", [128, 2, D])
        value_b = sb("value_b", [128, D])
        gate_bias = sb("gate_bias", [128, E])
        eye_s = sb("eye_s", [128, 128])
        eye16 = sb("eye16", [128, 128], F16)
        shift_s = sb("shift_s", [128, 128])
        w2_s = sb("w2_s", [128, NE, D])
        AW = 128 + D
        attn_hi = sb("attn_hi", [128, 3, AW], F16)
        attn_lo = sb("attn_lo", [128, 2, AW], F16)
        gate_hi = sb("gate_hi", [128, 3, E], F16)
        gate_lo = sb("gate_lo", [128, 2, E], F16)
        w1_hi = sb("w1_hi", [128, 3, NE * I], F16)
        w1_lo = sb("w1_lo", [128, 2, NE * I], F16)
        w3_hi = sb("w3_hi", [128, 3, NE * I], F16)
        w3_lo = sb("w3_lo", [128, 2, NE * I], F16)
        head_hi = sb("head_hi", [128, NH, 128], F16)
        head_lo = sb("head_lo", [128, NH, 128], F16)
        stage = sb("stage", [128, 3 * NE * I])
        gate_raw = sb("gate_raw", [128, 3, E])
        head_raw = stage[:, 0:NH * 128].rearrange("p (h s) -> p h s", h=NH)
        core_raw = stage[:, NH * 128:NH * 128 + 128]
        head_sum = stage[:, NH * 128 + 128:NH * 128 + 256]
        NSC = 6
        BASIS, VALUE, GATE, HEADS, W1, W3 = range(NSC)
        amax = sb("amax", [128, NSC])
        amax_all = sb("amax_all", [128, NSC])
        power = sb("power", [128, NSC])
        inverse = sb("inverse", [128, NSC])
        exp_scale = sb("exp_scale", [128, 1])
        gate_scale = sb("gate_scale", [128, 1])
        eps = sb("eps", [128, 1])
        minus_half = sb("minus_half", [128, 1])
        zero = sb("zero", [128, 1])
        unshift = sb("unshift", [128, 1])

        pairs = sb("pairs", [128, 2, 2, D + 1])
        wins = sb("wins", [P, 2, PL, D])
        xT = sb("xT", [128, 2, 4 * 128])
        th = sb("th", [128, 2, 2 * D])
        score = sb("score", [128, 2, 2])
        win_max = sb("win_max", [P, 1])
        win_d = sb("win_d", [P, PL])
        win_e = sb("win_e", [P, PL])
        win_z = sb("win_z", [P, 1])
        win_r = sb("win_r", [P, 1])
        win_w = sb("win_w", [P, 2, PL])
        half = sb("half", [P, 2, D])
        pooled = sb("pooled", [P, 2, D + 1])
        pooledT = sb("pooledT", [128, 2, 2 * P])
        res = sb("res", [P, B, D])
        stats = sb("stats", [P, 2, 6])
        mv = sb("mv", [P, 2, 2])
        after_stats = sb("after_stats", [P, 1])
        rstd = sb("rstd", [P, 2, 1])
        vpe = sb("vpe", [P, 2, 1])
        xn = sb("xn", [P, 2, D])
        z1 = sb("z1", [P, 2, 2 * D], F16)
        z2 = sb("z2", [P, 2, 2 * D], F16)
        z1T = sb("z1T", [128, 2, 3, P], F16)
        z2T = sb("z2T", [128, B, 3, P], F16)
        lat_a = sb("lat_a", [128, 2, P], F16)
        lat_b = sb("lat_b", [128, 2, P], F16)
        vals = sb("vals", [P, 2, NH, HV])
        q_a = sb("q_a", [128, 2, NH * P], F16)
        attn_raw = q_a[:].rearrange("p a n -> p (a n)").bitcast(F32)[:, 0:3 * AW].rearrange("p (a n) -> p a n", a=3)
        q_b = sb("q_b", [128, 2, NH * P], F16)
        row_max = sb("row_max", [P, 2, NH])
        neg_max = sb("neg_max", [P, NH])
        max_hl = sb("max_hl", [P, 2, 2 * NH], F16)
        max_hlT = sb("max_hlT", [2 * NH, 2, P], F16)
        probs = sb("probs", [P, 2, UW])
        ctxT = sb("ctxT", [128, 2, NU * P])
        recip = sb("recip", [P, NH])
        att = sb("att", [P, 2, D])
        logits = sb("logits", [P, B, E])
        choice = logits
        silu = q_a[:].rearrange("p a n -> p (a n)").bitcast(F32)[:, 0:2 * TB * P].rearrange("p (a n) -> p a n", a=2)
        inner = q_b[:].rearrange("p a n -> p (a n)").bitcast(F32)[:, 0:2 * TB * P].rearrange("p (a n) -> p a n", a=2)

        tok_bank, pool_bank, lat_bank, turn_bank = (bank(n) for n in ("tok_b", "pool_b", "lat_b_", "turn_b"))
        q_bank, max_bank, s_bank, ctx_bank = (bank(n) for n in ("q_bank", "max_b", "s_bank", "ctx_b"))
        banks = [tok_bank, pool_bank, lat_bank, turn_bank, q_bank, max_bank, s_bank, ctx_bank]
        lat16 = lat_bank[:, :].bitcast(F16)
        turn16 = turn_bank[:, :].bitcast(F16)

        s = {n: sem(n) for n in (
            "tok_params", "attn_params", "head_params", "w1_params", "w3_params", "w2_params",
            "amax_part", "amax_done", "prep", "w_hi", "consts", "tok_ready", "attn_ready", "ffn_ready",
            "pairs_in", "wins_in", "max_rows_in",
            "xT_psum", "tok_psum", "win_psum", "pooledT_psum", "h_psum", "z1T_psum", "lat_psum",
            "val_psum", "q_psum", "max_psum", "s_psum", "ctx_psum", "maxT_psum", "att_psum",
            "z2T_psum", "logit_psum",
            "xT_copied", "tanh_done", "win_exp", "pooledT_copied", "h_copied", "lat_hi", "q_hi",
            "exp_done", "ctxT_copied", "z2T_copied",
            "score_part", "score_done", "win_max_done", "win_d_done", "win_z_done", "win_r_done",
            "win_w_done", "stats1", "mv1", "xn1", "stats2", "mv2", "xn2", "z1T_copied", "lat_lo",
            "val_done", "q_lo", "max_done", "maxT_copied", "recip_done", "att_done", "logits_copied",
            "vpe1", "rstd1", "z1_hi", "z1_done", "vpe2", "rstd2", "z2_hi", "z2_done", "lat_b_done",
            "prod_done", "half_done", "pooled_done", "neg_done", "max_hi", "max_hl_done", "res_done",
            "gate_tanh", "gate_step", "h1_psum", "h3_psum", "silu_done", "inner_done", "y_psum",
            "acc_done", "stored",
        )}

        block = ctx.enter_context(nc.Block())

        @block.sync
        def _(sp):
            for dst, src in ((w_tok_s[:], w_tok), (b_tok_s[96:128, :], b_tok), (v_tok_s[:], v_tok),
                             (vb_s[:], vb_tok), (p_tok_s[:], p_tok), (eye_s[:], eye), (shift_s[:], shift)):
                sp.dma_start(dst, src).then_inc(s["tok_params"], 16)
            for dst, src in ((attn_raw, attn_w), (value_b[:], attn_vb), (gate_raw[:], gate_w),
                             (gate_bias[:], gate_b)):
                sp.dma_start(dst, src).then_inc(s["attn_params"], 16)
            sp.dma_start(head_raw, head_res).then_inc(s["head_params"], 16)
            sp.dma_start(core_raw, core).then_inc(s["head_params"], 16)
            sp.dma_start(w2_s[:], w2).then_inc(s["w2_params"], 16)

            def step(it, par):
                n = it
                if on(n):
                    if later(n, 1):
                        sp.wait_ge(s["xT_psum"], n)
                    sp.dma_start(pairs[:, par, :, 0:D],
                                 x[n, :, :].rearrange("(q c) d -> q c d", c=2)).then_inc(s["pairs_in"], 16)
                j = it - 4
                if on(j):
                    sp.wait_ge(s["maxT_copied"], j + 1)
                    sp.dma_start(q_b[R:R + 2, par, :].rearrange("r (h n) -> r h n", h=NH),
                                 max_hlT[:, par, :]).then_inc(s["max_rows_in"], 16)
                if on(n):
                    if later(n, 1):
                        sp.wait_ge(s["half_done"], n)
                    sp.dma_start(wins[:, par, :, :].rearrange("p l d -> p (l d)"),
                                 windows(x)[n, :, :]).then_inc(s["wins_in"], 16)
                if isinstance(it, int) and it == 1:
                    sp.wait_ge(s["attn_ready"], 1)
                    sp.dma_start(stage[:], w1).then_inc(s["w1_params"], 16)
                if isinstance(it, int) and it == 3:
                    sp.wait_ge(s["ffn_ready"], 1)
                    sp.dma_start(stage[:], w3).then_inc(s["w3_params"], 16)

            walk(sp, step)
            with sp.Fori(0, NG) as g:
                sp.wait_ge(s["acc_done"], NE * (g + 1))
                sp.dma_start(out[bass.ts(g, TB), :, :].rearrange("b p d -> p b d"),
                             res[:, bass.ts(g, TB), :]).then_inc(s["stored"], 16)
            sp.wait_ge(s["stored"], 16 * NG)

        @block.gpsimd
        def _(pool):
            for m, (place, value) in enumerate((
                    (pairs[:, :, :, D:D + 1], 1.0), (pooled[:, :, D:D + 1], 1.0), (vals[:, :, :, HD:HV], 1.0),
                    (q_b[R:128, :, :], 0.0), (lat_b[R:128, :, :], 0.0), (lat_b[R:R + 2, :, :], SHIFT),
                    (eps[:], 1e-5), (minus_half[:], -0.5), (zero[:], 0.0), (unshift[:], -1.0 / SHIFT))):
                pool.memset(place, value).then_inc(s["consts"], 1)
                pool.wait_ge(s["consts"], m + 1)
            pool.wait_ge(s["amax_part"], 1)
            pool.partition_all_reduce(amax_all[:, 0:4], amax[:, 0:4], 128,
                                      bass.bass_isa.ReduceOp.absmax).then_inc(s["amax_done"], 1)

            def norm_scale(n, k, mv_done, vpe_done, rstd_done):
                pool.wait_ge(mv_done, n + 1)
                pool.tensor_tensor(vpe[:, k, :], mv[:, k, 1:2], eps[0:P, :], ALU.add).then_inc(vpe_done, 1)
                pool.wait_ge(vpe_done, n + 1)
                pool.tensor_tensor(rstd[:, k, :], vpe[:, k, :], minus_half[0:P, :],
                                   ALU.pow).then_inc(rstd_done, 1)

            def split_norm(n, k, par, z, xn_done, hi_done, lo_done, readers):
                pool.wait_ge(xn_done, n + 1)
                if later(n, 2):
                    pool.wait_ge(readers, n - 1)
                pool.tensor_tensor(z[:, par, 0:D], xn[:, k, :], zero[0:P, :].to_broadcast([P, D]),
                                   ALU.add).then_inc(hi_done, 1)
                pool.wait_ge(hi_done, n + 1)
                pool.tensor_tensor(z[:, par, D:2 * D], xn[:, k, :], z[:, par, 0:D],
                                   ALU.subtract).then_inc(lo_done, 1)

            def step(it, par):
                t, a, z, j, k, l = (it - m for m in range(1, 7))
                odd = 1 - par
                if on(l):
                    norm_scale(l, 1, s["mv2"], s["vpe2"], s["rstd2"])
                    split_norm(l, 1, par, z2, s["xn2"], s["z2_hi"], s["z2_done"], s["z2T_psum"])
                if on(j):
                    pool.wait_ge(s["max_done"], NU * (j + 1))
                    pool.tensor_tensor(neg_max[:], row_max[:, par, :], unshift[0:P, :].to_broadcast([P, NH]),
                                       ALU.mult).then_inc(s["neg_done"], 1)
                    pool.wait_ge(s["neg_done"], j + 1)
                    if later(j, 2):
                        pool.wait_ge(s["maxT_psum"], j - 1)
                    pool.tensor_tensor(max_hl[:, par, 0:NH], neg_max[:], zero[0:P, :].to_broadcast([P, NH]),
                                       ALU.add).then_inc(s["max_hi"], 1)
                    pool.wait_ge(s["max_hi"], j + 1)
                    pool.tensor_tensor(max_hl[:, par, NH:2 * NH], neg_max[:], max_hl[:, par, 0:NH],
                                       ALU.subtract).then_inc(s["max_hl_done"], 1)
                if on(a):
                    norm_scale(a, 0, s["mv1"], s["vpe1"], s["rstd1"])
                    split_norm(a, 0, par, z1, s["xn1"], s["z1_hi"], s["z1_done"], s["z1T_psum"])
                if on(k):
                    pool.wait_ge(s["att_done"], k + 1)
                    pool.tensor_tensor(res[:, k, :], res[:, k, :], att[:, odd, :],
                                       ALU.add).then_inc(s["res_done"], 1)
                if on(z):
                    pool.wait_ge(s["lat_hi"], z + 1)
                    if later(z, 2):
                        pool.wait_ge(s["s_psum"], NU * (z - 1))
                    pool.tensor_tensor(lat_b[0:R, odd, :], lat_a[0:R, odd, :], zero[0:R, :].to_broadcast([R, P]),
                                       ALU.add).then_inc(s["lat_b_done"], 1)
                if on(t):
                    pool.wait_ge(s["win_w_done"], t + 1)
                    pool.wait_ge(s["wins_in"], 16 * (t + 1))
                    pool.tensor_tensor(wins[:, odd, :, :], wins[:, odd, :, :],
                                       win_w[:, odd, :].unsqueeze(2).to_broadcast([P, PL, D]),
                                       ALU.mult).then_inc(s["prod_done"], 1)
                    pool.wait_ge(s["prod_done"], t + 1)
                    if later(t, 1):
                        pool.wait_ge(s["pooled_done"], t)
                    pool.tensor_tensor(half[:], wins[:, odd, 0:2, :], wins[:, odd, 2:4, :],
                                       ALU.add).then_inc(s["half_done"], 1)
                    pool.wait_ge(s["half_done"], t + 1)
                    if later(t, 2):
                        pool.wait_ge(s["pooledT_psum"], t - 1)
                    pool.tensor_tensor(pooled[:, odd, 0:D], half[:, 0, :], half[:, 1, :],
                                       ALU.add).then_inc(s["pooled_done"], 1)
                if isinstance(it, int) and it in (1, 3):
                    c = 4 + it // 2
                    pool.wait_ge(s["amax_part"], c - 2)
                    pool.partition_all_reduce(amax_all[:, c:c + 1], amax[:, c:c + 1], 128,
                                              bass.bass_isa.ReduceOp.absmax).then_inc(s["amax_done"], 1)

            walk(pool, step)

        @block.scalar
        def _(act):
            def step(it, par):
                t, a, z, j, k, l = (it - m for m in range(1, 7))
                odd = 1 - par

                def query_hi(u):
                    if not on(j):
                        return
                    act.wait_ge(s["q_psum"], NU * j + u + 1)
                    act.activation(q_a[:, par, u * UW:(u + 1) * UW], q_bank[:, 0:UW],
                                   ACT.Copy).then_inc(s["q_hi"], 1)

                def exps(u):
                    if not on(k):
                        return
                    act.wait_ge(s["s_psum"], NU * k + u + 1)
                    if later(k, 1) or u >= 2:
                        act.wait_ge(s["ctx_psum"], NU * k + u - 1)
                    act.activation(probs[:, (odd + u) % 2, :], s_bank[0:P, 0:UW], ACT.Exp,
                                   scale=exp_scale[0:P, :]).then_inc(s["exp_done"], 1)

                if on(t):
                    act.wait_ge(s["xT_psum"], t + 1)
                    if later(t, 2):
                        act.wait_ge(s["tok_psum"], t - 1)
                    act.activation(xT[:, odd, :], tok_bank[:, :], ACT.Copy).then_inc(s["xT_copied"], 1)
                query_hi(0)
                if on(t):
                    act.wait_ge(s["tok_psum"], t + 1)
                    if later(t, 2):
                        act.wait_ge(s["score_done"], t - 1)
                    act.activation(th[:, odd, :], tok_bank[:, 0:2 * D], ACT.Tanh).then_inc(s["tanh_done"], 1)
                query_hi(1)
                if it_first(it, 5):
                    act.wait_ge(s["attn_ready"], 1)
                exps(0)
                if on(t):
                    act.wait_ge(s["win_d_done"], t + 1)
                    act.activation(win_e[:], win_d[:], ACT.Exp).then_inc(s["win_exp"], 1)
                if on(l):
                    act.wait_ge(s["z2T_psum"], l + 1)
                    act.activation(z2T[:, l, :, :], turn16[:, 0:384].rearrange("p (c n) -> p c n", c=3)[:, :, 0:P],
                                   ACT.Copy).then_inc(s["z2T_copied"], 1)
                query_hi(2)
                exps(1)
                if on(a):
                    act.wait_ge(s["pooledT_psum"], a + 1)
                    if later(a, 2):
                        act.wait_ge(s["h_psum"], a - 1)
                    act.activation(pooledT[:, par, :], pool_bank[:, 0:2 * P],
                                   ACT.Copy).then_inc(s["pooledT_copied"], 1)
                exps(2)
                if on(a):
                    act.wait_ge(s["h_psum"], a + 1)
                    act.activation(res[:, a, :], pool_bank[0:P, 0:D], ACT.Copy).then_inc(s["h_copied"], 1)
                if on(k):
                    act.wait_ge(s["ctx_psum"], NU * (k + 1))
                    if later(k, 2):
                        act.wait_ge(s["att_psum"], k - 1)
                    act.activation(ctxT[:, odd, :], ctx_bank[:, 0:NU * P],
                                   ACT.Copy).then_inc(s["ctxT_copied"], 1)
                if on(z):
                    act.wait_ge(s["lat_psum"], z + 1)
                    if later(z, 2):
                        act.wait_ge(s["s_psum"], NU * (z - 1))
                    act.activation(lat_a[:, odd, :], lat_bank[:, 0:P], ACT.Copy).then_inc(s["lat_hi"], 1)

            walk(act, step)
            act.wait_ge(s["logits_copied"], B)
            act.activation(logits[:], logits[:], ACT.Tanh, scale=gate_scale[0:P, :]).then_inc(s["gate_tanh"], 1)

            def silus(n, half_):
                act.wait_ge(s["h1_psum"], n + 1)
                if not isinstance(n, int) or n >= 2:
                    act.wait_ge(s["inner_done"], n - 1)
                act.activation(silu[:, half_, :], banks[half_][:, 0:TB * P], ACT.Silu,
                               scale=power[:, W1:W1 + 1]).then_inc(s["silu_done"], 1)

            for m in range(2 * NE):
                silus(m, m % 2)
            with act.Fori(1, NG // 2) as q:
                for m in range(2 * NE):
                    silus(2 * NE * q + m, m % 2)

        @block.vector
        def _(dve):
            prepared = [0]

            def link(ins):
                prepared[0] += 1
                ins.then_inc(s["prep"], 1)
                dve.wait_ge(s["prep"], prepared[0])

            def scale_of(c0, c1):
                link(dve.tensor_scalar(amax_all[:, c0:c1], amax_all[:, c0:c1], 2.0 ** -100, None, ALU.max))
                link(dve.tensor_scalar(power[:, c0:c1].bitcast(I32), amax_all[:, c0:c1].bitcast(I32),
                                       0x7F800000, None, ALU.bitwise_and))
                link(dve.reciprocal(inverse[:, c0:c1], power[:, c0:c1]))

            def split(hi, lo, raw, lo_raw, hi_part, c):
                link(dve.tensor_scalar(hi, raw, inverse[:, c:c + 1], None, ALU.mult))
                link(dve.scalar_tensor_tensor(lo, lo_raw, inverse[:, c:c + 1], hi_part, ALU.mult, ALU.subtract))

            link(dve.memset(ctx_bank[:, :], 0.0))
            dve.wait_ge(s["tok_params"], 16 * 7)
            link(dve.tensor_copy(eye16[:], eye_s[:]))
            dve.tensor_tensor(w_tok_s[96:128, 1, :], w_tok_s[96:128, 1, :], b_tok_s[96:128, :],
                              ALU.add).then_inc(s["tok_ready"], 1)

            dve.wait_ge(s["attn_params"], 16 * 4)
            dve.wait_ge(s["head_params"], 16 * 2)
            link(dve.tensor_reduce(head_sum, head_raw.rearrange("p h s -> p s h"), AX.X, ALU.add))
            link(dve.tensor_tensor(core_raw, core_raw, head_sum, ALU.subtract))
            link(dve.tensor_scalar(core_raw, core_raw, 1.0 / NH, None, ALU.mult))
            link(dve.tensor_tensor(head_raw, head_raw, core_raw.unsqueeze(1).to_broadcast([128, NH, 128]), ALU.add))

            def biggest(c, src, axis):
                return dve.tensor_reduce(amax[:, c:c + 1], src, axis, ALU.max, apply_absolute_value=True)

            link(biggest(BASIS, attn_raw[:, 0:2, 0:128], AX.XY))
            link(biggest(VALUE, attn_raw[:, 0:2, 128:AW], AX.XY))
            link(biggest(GATE, gate_raw[:, 0:2, :], AX.XY))
            biggest(HEADS, head_raw, AX.XY).then_inc(s["amax_part"], 1)
            dve.wait_ge(s["amax_done"], 1)
            scale_of(0, 4)
            split(attn_hi[:, :, 0:128], attn_lo[:, :, 0:128], attn_raw[:, :, 0:128],
                  attn_raw[:, 0:2, 0:128], attn_hi[:, 0:2, 0:128], BASIS)
            split(attn_hi[:, :, 128:AW], attn_lo[:, :, 128:AW], attn_raw[:, :, 128:AW],
                  attn_raw[:, 0:2, 128:AW], attn_hi[:, 0:2, 128:AW], VALUE)
            split(gate_hi[:], gate_lo[:], gate_raw[:], gate_raw[:, 0:2, :], gate_hi[:, 0:2, :], GATE)
            split(head_hi[:], head_lo[:], head_raw, head_raw, head_hi[:], HEADS)
            link(dve.tensor_tensor(exp_scale[:], power[:, BASIS:BASIS + 1], power[:, BASIS:BASIS + 1], ALU.mult))
            link(dve.tensor_tensor(exp_scale[:], exp_scale[:], power[:, HEADS:HEADS + 1], ALU.mult))
            link(dve.tensor_scalar(exp_scale[:], exp_scale[:], R ** -0.5, None, ALU.mult))
            dve.tensor_scalar(gate_scale[:], power[:, GATE:GATE + 1], 0.5, None,
                              ALU.mult).then_inc(s["attn_ready"], 1)

            def prepare_ffn(c, params, hi, lo):
                dve.wait_ge(params, 16)
                raw = stage[:].rearrange("p (a n) -> p a n", a=3)
                biggest(c, raw[:, 0:2, :], AX.XY).then_inc(s["amax_part"], 1)
                dve.wait_ge(s["amax_done"], c - 2)
                scale_of(c, c + 1)
                for tile in range(3):
                    dve.tensor_scalar(hi[:, tile, :], raw[:, tile, :], inverse[:, c:c + 1], None,
                                      ALU.mult).then_inc(s["w_hi"], 1)
                    dve.wait_ge(s["w_hi"], 3 * (c - W1) + tile + 1)
                for tile in range(2):
                    last = dve.scalar_tensor_tensor(lo[:, tile, :], raw[:, tile, :], inverse[:, c:c + 1],
                                                    hi[:, tile, :], ALU.mult, ALU.subtract)
                last.then_inc(s["ffn_ready"], 1)

            def norm_stats(n, k, stats_done):
                dve.bn_stats(stats[:, k, :], res[:, n, :]).then_inc(stats_done, 1)
                dve.wait_ge(stats_done, n + 1)
                dve.memset(after_stats[:], 0.0)

            def norm_mean(k, mv_done):
                dve.bn_aggr(mv[:, k, :], stats[:, k, :]).then_inc(mv_done, 1)

            def normed(n, k, rstd_done, xn_done, split_done):
                dve.wait_ge(rstd_done, n + 1)
                if later(n, 1):
                    dve.wait_ge(split_done, n)
                dve.tensor_scalar(xn[:, k, :], res[:, n, :], mv[:, k, 0:1], rstd[:, k, :],
                                  ALU.subtract, ALU.mult).then_inc(xn_done, 1)

            def step(it, par):
                t, a, z, j, k, l = (it - m for m in range(1, 7))
                odd = 1 - par

                def query_lo(u):
                    if not on(j):
                        return
                    dve.wait_ge(s["q_hi"], NU * j + u + 1)
                    dve.tensor_tensor(q_b[0:R, par, u * UW:(u + 1) * UW], q_bank[0:R, 0:UW],
                                      q_a[0:R, par, u * UW:(u + 1) * UW], ALU.subtract).then_inc(s["q_lo"], 1)

                def maxima(u):
                    if not on(j):
                        return
                    dve.wait_ge(s["max_psum"], NU * j + u + 1)
                    if u == 0 and later(j, 2):
                        dve.wait_ge(s["neg_done"], j - 1)
                    dve.tensor_reduce(row_max[:, par, u * U:(u + 1) * U],
                                      max_bank[0:P, 0:UW].rearrange("p (h m) -> p h m", h=U),
                                      AX.X, ALU.max).then_inc(s["max_done"], 1)

                if on(l):
                    dve.wait_ge(s["res_done"], l + 1)
                    norm_stats(l, 1, s["stats2"])
                    norm_mean(1, s["mv2"])
                    normed(l, 1, s["rstd2"], s["xn2"], s["z2_done"])
                query_lo(0)
                if on(t):
                    dve.wait_ge(s["tanh_done"], t + 1)
                    if later(t, 2):
                        dve.wait_ge(s["win_psum"], t - 1)
                    for c in range(2):
                        dve.tensor_tensor_reduce(
                            out=th[:, odd, c * D:(c + 1) * D], in0=th[:, odd, c * D:(c + 1) * D], in1=v_tok_s[:], scale=1.0,
                            scalar=vb_s[:, 0:1], op0=ALU.mult, op1=ALU.add,
                            accum_out=score[:, odd, c:c + 1]).then_inc(s["score_part" if c == 0 else "score_done"], 1)
                        if c == 0:
                            dve.wait_ge(s["score_part"], t + 1)
                maxima(0)
                query_lo(1)
                if on(t):
                    dve.wait_ge(s["win_psum"], t + 1)
                    dve.tensor_reduce(win_max[:], pool_bank[0:P, 0:PL], AX.X, ALU.max).then_inc(s["win_max_done"], 1)
                    dve.wait_ge(s["win_max_done"], t + 1)
                    dve.tensor_scalar(win_d[:], pool_bank[0:P, 0:PL], win_max[:], None,
                                      ALU.subtract).then_inc(s["win_d_done"], 1)
                maxima(1)
                if on(t):
                    dve.wait_ge(s["win_exp"], t + 1)
                    dve.tensor_reduce(win_z[:], win_e[:], AX.X, ALU.add).then_inc(s["win_z_done"], 1)
                    dve.wait_ge(s["win_z_done"], t + 1)
                    dve.reciprocal(win_r[:], win_z[:]).then_inc(s["win_r_done"], 1)
                    dve.wait_ge(s["win_r_done"], t + 1)
                    if later(t, 2):
                        dve.wait_ge(s["prod_done"], t - 1)
                    dve.tensor_scalar(win_w[:, odd, :], win_e[:], win_r[:], None,
                                      ALU.mult).then_inc(s["win_w_done"], 1)
                query_lo(2)
                maxima(2)
                if on(l):
                    dve.wait_ge(s["logit_psum"], l + 1)
                    dve.tensor_copy(logits[:, l, :], turn_bank[0:P, 0:E]).then_inc(s["logits_copied"], 1)
                if on(a):
                    dve.wait_ge(s["h_copied"], a + 1)
                    norm_stats(a, 0, s["stats1"])
                    norm_mean(0, s["mv1"])
                if on(j):
                    dve.wait_ge(s["maxT_psum"], j + 1)
                    if later(j, 2):
                        dve.wait_ge(s["max_rows_in"], 16 * (j - 1))
                    dve.tensor_copy(max_hlT[:, par, :], turn16[0:2 * NH, 0:P]).then_inc(s["maxT_copied"], 1)
                if on(z):
                    dve.wait_ge(s["z1T_psum"], z + 1)
                    dve.tensor_copy(z1T[:, odd, :, :],
                                    lat16[:, 0:384].rearrange("p (c n) -> p c n", c=3)[:, :, 0:P]
                                    ).then_inc(s["z1T_copied"], 1)
                if on(a):
                    normed(a, 0, s["rstd1"], s["xn1"], s["z1_done"])
                if on(k):
                    dve.wait_ge(s["att_psum"], k + 1)
                    att_ps = turn_bank[0:P, 0:NU * 128].rearrange("p (h d) -> p h d", d=32)
                    dve.reciprocal(recip[:], att_ps[:, :, HD]).then_inc(s["recip_done"], 1)
                    dve.wait_ge(s["recip_done"], k + 1)
                    if later(k, 2):
                        dve.wait_ge(s["res_done"], k - 1)
                    dve.tensor_tensor(att[:, odd, :].rearrange("p (h d) -> p h d", d=HD), att_ps[:, :, 0:HD],
                                      recip[:].unsqueeze(2).to_broadcast([P, NH, HD]),
                                      ALU.mult).then_inc(s["att_done"], 1)
                if on(z):
                    dve.wait_ge(s["lat_hi"], z + 1)
                    dve.tensor_tensor(lat_a[R:128, odd, :], lat_bank[R:128, 0:P], lat_a[R:128, odd, :],
                                      ALU.subtract).then_inc(s["lat_lo"], 1)
                    dve.wait_ge(s["val_psum"], z + 1)
                    dve.scalar_tensor_tensor(
                        vals[:, odd, :, 0:HD], lat_bank[0:P, 128:128 + D].rearrange("p (h d) -> p h d", d=HD),
                        power[0:P, VALUE:VALUE + 1], value_b[0:P, :].rearrange("p (h d) -> p h d", d=HD),
                        ALU.mult, ALU.add).then_inc(s["val_done"], 1)
                if isinstance(it, int) and it == 1:
                    prepare_ffn(W1, s["w1_params"], w1_hi, w1_lo)
                if isinstance(it, int) and it == 3:
                    prepare_ffn(W3, s["w3_params"], w3_hi, w3_lo)

            walk(dve, step)

            sizes = (("sig", E), ("biased", E), ("masked", E), ("rank", E), ("cmp", E),
                     ("group", G), ("group_rank", G), ("group_cmp", G), ("norm", 1))
            room, at = {}, 0
            for name, width in sizes:
                room[name] = stage[0:P, at:at + B * width].rearrange("p (b e) -> p b e", e=width)
                at += B * width
            sig, biased, masked, rank, comp = (room[n] for n in ("sig", "biased", "masked", "rank", "cmp"))
            group, group_rank, group_cmp, norm = (room[n] for n in ("group", "group_rank", "group_cmp", "norm"))
            steps = [0]

            def then(ins):
                steps[0] += 1
                ins.then_inc(s["gate_step"], 1)
                dve.wait_ge(s["gate_step"], steps[0])

            def ranks(out_, val, tmp, n):
                for e in range(n):
                    then(dve.memset(out_[:, :, e:e + 1], float(n - 1 - e)))
                for d in range(1, n):
                    then(dve.tensor_tensor(tmp[:, :, 0:n - d], val[:, :, 0:n - d], val[:, :, d:n], ALU.is_ge))
                    then(dve.tensor_tensor(out_[:, :, d:n], out_[:, :, d:n], tmp[:, :, 0:n - d], ALU.add))
                    then(dve.tensor_tensor(out_[:, :, 0:n - d], out_[:, :, 0:n - d], tmp[:, :, 0:n - d], ALU.subtract))

            dve.wait_ge(s["gate_tanh"], 1)
            then(dve.tensor_scalar(sig, logits[:], 0.5, 0.5, ALU.mult, ALU.add))
            then(dve.tensor_tensor(biased, sig, gate_bias[0:P, :].unsqueeze(1).to_broadcast([P, B, E]), ALU.add))
            pair = biased.rearrange("p b (g e) -> p b g e", e=E // G)
            then(dve.tensor_tensor(group, pair[:, :, :, 0], pair[:, :, :, 1], ALU.add))
            ranks(group_rank, group, group_cmp, G)
            then(dve.tensor_scalar(group_cmp, group_rank, 1.5, None, ALU.is_lt))
            then(dve.tensor_scalar(group, group_cmp, 1e30, -1e30, ALU.mult, ALU.add))
            in_pairs = masked.rearrange("p b (g e) -> p (b g) e", e=E // G)
            then(dve.tensor_tensor(in_pairs, biased.rearrange("p b (g e) -> p (b g) e", e=E // G),
                                   group_cmp.rearrange("p b g -> p (b g)").unsqueeze(2)
                                   .to_broadcast([P, B * G, E // G]), ALU.mult))
            then(dve.tensor_tensor(in_pairs, in_pairs,
                                   group.rearrange("p b g -> p (b g)").unsqueeze(2)
                                   .to_broadcast([P, B * G, E // G]), ALU.add))
            ranks(rank, masked, comp, E)
            then(dve.scalar_tensor_tensor(masked, rank, TOPK - 0.5, sig, ALU.is_lt, ALU.mult))
            then(dve.tensor_reduce(norm[:, :, 0], masked, AX.X, ALU.add))
            then(dve.tensor_scalar(norm, norm, 1e-6, None, ALU.add))
            then(dve.reciprocal(norm, norm))
            then(dve.tensor_tensor(choice[:], masked, norm.to_broadcast([P, B, E]), ALU.mult))

            def inners(n, half_):
                dve.wait_ge(s["silu_done"], n + 1)
                dve.wait_ge(s["h3_psum"], n + 1)
                if not isinstance(n, int) or n >= 2:
                    dve.wait_ge(s["y_psum"], n - 1)
                dve.scalar_tensor_tensor(inner[:, half_, :], banks[2 + half_][:, 0:TB * P], power[:, W3:W3 + 1],
                                         silu[:, half_, :], ALU.mult, ALU.mult).then_inc(s["inner_done"], 1)

            def accumulate(n, g, e, half_):
                dve.wait_ge(s["y_psum"], n + 1)
                if not isinstance(n, int) or n >= 1:
                    dve.wait_ge(s["acc_done"], n)
                for b in range(TB):
                    y = banks[4 + 2 * half_ + b // 2][0:P, (b % 2) * 256:(b % 2) * 256 + D]
                    r = res[:, TB * g + b, :]
                    if e == E:
                        ins = dve.tensor_tensor(r, y, r, ALU.add)
                    else:
                        ins = dve.scalar_tensor_tensor(r, y, choice[:, TB * g + b, e:e + 1], r, ALU.mult, ALU.add)
                ins.then_inc(s["acc_done"], 1)

            def two_groups(q):
                for m in range(2 * NE):
                    n = 2 * NE * q + m
                    if m + 1 < 2 * NE:
                        inners(n + 1, (m + 1) % 2)
                    elif not (isinstance(q, int) and q == NG // 2 - 1):
                        inners(n + 1, 0)
                    accumulate(n, 2 * q + m // NE, order[m % NE], m % 2)

            order = [E] + list(range(E))
            inners(0, 0)
            two_groups(0)
            with dve.Fori(1, NG // 2 - 1) as q:
                two_groups(q)
            two_groups(NG // 2 - 1)

        @block.tensor
        def _(pe):
            def mm(out_, lhsT, rhs, start=True, stop=True):
                return pe.matmul(out_, lhsT, rhs, start=start, stop=stop)

            def split_product(out_, left, right):
                terms = [(0, 0), (1, 0), (2, 0), (0, 1), (1, 1)]
                for m, (tile, lo) in enumerate(terms):
                    last = mm(out_, left(tile, lo), right(tile, lo), start=(m == 0), stop=(m == len(terms) - 1))
                return last

            def norm_transposes(dst16, z, par):
                for c in range(3):
                    last = pe.transpose(dst16[:, c * 128:c * 128 + P], z[:, par, c * 128:(c + 1) * 128],
                                        eye16[0:P, 0:P])
                return last

            def step(it, par):
                t, a, z, j, k, l = (it - m for m in range(1, 7))
                odd = 1 - par

                def queries(u):
                    if not on(j):
                        return
                    if later(j, 1) or u:
                        pe.wait_ge(s["q_lo"], NU * j + u)
                    for h in range(U):
                        o = q_bank[:, h * P:(h + 1) * P]
                        mm(o, head_hi[:, u * U + h, :], lat_a[:, par, :], stop=False)
                        last = mm(o, head_lo[:, u * U + h, :], lat_a[:, par, :], start=False)
                    last.then_inc(s["q_psum"], 1)

                def max_scores(u):
                    if not on(j):
                        return
                    pe.wait_ge(s["q_hi"], NU * j + u + 1)
                    if later(j, 1) or u:
                        pe.wait_ge(s["max_done"], NU * j + u)
                    for h in range(U):
                        c = (u * U + h) * P
                        last = mm(max_bank[0:P, h * P:(h + 1) * P], q_a[:, par, c:c + P], lat_a[:, par, :])
                    last.then_inc(s["max_psum"], 1)

                def scores(u):
                    if not on(k):
                        return
                    if u == 0:
                        pe.wait_ge(s["max_rows_in"], 16 * (k + 1))
                        pe.wait_ge(s["q_lo"], NU * (k + 1))
                    if later(k, 1) or u:
                        pe.wait_ge(s["exp_done"], NU * k + u)
                    cols = slice(u * UW, (u + 1) * UW)
                    mm(s_bank[0:P, 0:UW], lat_a[:, odd, :], q_a[:, odd, cols], stop=False)
                    mm(s_bank[0:P, 0:UW], lat_b[:, odd, :], q_b[:, odd, cols],
                       start=False).then_inc(s["s_psum"], 1)

                def weighted(u):
                    if not on(k):
                        return
                    pe.wait_ge(s["exp_done"], NU * k + u + 1)
                    if u == 0 and later(k, 1):
                        pe.wait_ge(s["ctxT_copied"], k)
                    for h in range(U):
                        last = pe.matmul(ctx_bank[32 * h:32 * h + HV, u * P:(u + 1) * P],
                                         vals[:, odd, u * U + h, :], probs[:, (odd + u) % 2, h * P:(h + 1) * P],
                                         start=True, stop=True, tile_position=(0, 32 * h))
                    last.then_inc(s["ctx_psum"], 1)

                if on(t):
                    if it_first(it, 1):
                        pe.wait_ge(s["consts"], 10)
                        pe.wait_ge(s["tok_ready"], 1)
                    pe.wait_ge(s["pairs_in"], 16 * (t + 1))
                    if later(t, 1):
                        pe.wait_ge(s["tanh_done"], t)
                    for c in range(2):
                        for tile, at in enumerate((0, CUT)):
                            o = (2 * c + tile) * 128
                            last = pe.transpose(tok_bank[:, o:o + 128], pairs[:, odd, c, at:at + 128], eye_s[:])
                    last.then_inc(s["xT_psum"], 1)
                queries(0)
                if on(t):
                    pe.wait_ge(s["xT_copied"], t + 1)
                    for c in range(2):
                        for tile in range(2):
                            o = (2 * c + tile) * 128
                            last = mm(tok_bank[:, c * D:(c + 1) * D], xT[:, odd, o:o + 128], w_tok_s[:, tile, :],
                                      start=(tile == 0), stop=(tile == 1))
                    last.then_inc(s["tok_psum"], 1)
                max_scores(0)
                queries(1)
                scores(0)
                if on(t):
                    pe.wait_ge(s["score_done"], t + 1)
                    if later(t, 2):
                        pe.wait_ge(s["h_copied"], t - 1)
                    mm(pool_bank[0:P, 0:2], eye_s[:, 0:P], score[:, odd, :])
                    mm(pool_bank[0:P, 2:4], shift_s[:, 0:P], score[:, odd, :]).then_inc(s["win_psum"], 1)
                max_scores(1)
                if on(l):
                    pe.wait_ge(s["z2_done"], l + 1)
                    pe.wait_ge(s["att_done"], l + 1)
                    norm_transposes(turn16, z2, par).then_inc(s["z2T_psum"], 1)
                queries(2)
                scores(1)
                weighted(0)
                max_scores(2)
                if on(a):
                    pe.wait_ge(s["pooled_done"], a + 1)
                    if on(t):
                        pe.wait_ge(s["win_d_done"], t + 1)
                    for tile, at in enumerate((0, CUT)):
                        last = pe.transpose(pool_bank[:, tile * P:(tile + 1) * P], pooled[:, par, at:at + 128],
                                            eye_s[0:P, 0:P])
                    last.then_inc(s["pooledT_psum"], 1)
                if on(l):
                    pe.wait_ge(s["z2T_copied"], l + 1)
                    split_product(turn_bank[0:P, 0:E], lambda tile, lo: z2T[:, l, tile, :],
                                  lambda tile, lo: (gate_lo if lo else gate_hi)[:, tile, :]
                                  ).then_inc(s["logit_psum"], 1)
                scores(2)
                weighted(1)
                if on(a):
                    pe.wait_ge(s["pooledT_copied"], a + 1)
                    for tile in range(2):
                        last = mm(pool_bank[0:P, 0:D], pooledT[:, par, tile * P:(tile + 1) * P], p_tok_s[:, tile, :],
                                  start=(tile == 0), stop=(tile == 1))
                    last.then_inc(s["h_psum"], 1)
                if on(j):
                    pe.wait_ge(s["max_hl_done"], j + 1)
                    if on(l):
                        pe.wait_ge(s["logits_copied"], l + 1)
                    elif later(j, 1):
                        pe.wait_ge(s["att_done" if on(k - 1) else "maxT_copied"], k if on(k - 1) else j)
                    pe.transpose(turn16[0:2 * NH, 0:P], max_hl[:, par, :], eye16[0:P, 0:P]).then_inc(s["maxT_psum"], 1)
                weighted(2)
                if on(z):
                    pe.wait_ge(s["z1_done"], z + 1)
                    if later(z, 1):
                        pe.wait_ge(s["val_done"], z)
                    norm_transposes(lat16, z1, odd).then_inc(s["z1T_psum"], 1)
                if on(k):
                    pe.wait_ge(s["ctxT_copied"], k + 1)
                    if on(j):
                        pe.wait_ge(s["maxT_copied"], j + 1)
                    elif on(l):
                        pe.wait_ge(s["logits_copied"], l + 1)
                    for u in range(NU):
                        last = pe.transpose(turn_bank[0:P, u * 128:(u + 1) * 128], ctxT[:, odd, u * P:(u + 1) * P],
                                            eye_s[:])
                    last.then_inc(s["att_psum"], 1)
                if on(z):
                    if it_first(it, 3):
                        pe.wait_ge(s["attn_ready"], 1)
                    pe.wait_ge(s["z1T_copied"], z + 1)
                    split_product(lat_bank[:, 0:P], lambda tile, lo: (attn_lo if lo else attn_hi)[:, tile, 0:128],
                                  lambda tile, lo: z1T[:, odd, tile, :]).then_inc(s["lat_psum"], 1)
                    pe.wait_ge(s["lat_lo"], z + 1)
                    split_product(lat_bank[0:P, 128:128 + D], lambda tile, lo: z1T[:, odd, tile, :],
                                  lambda tile, lo: (attn_lo if lo else attn_hi)[:, tile, 128:AW]
                                  ).then_inc(s["val_psum"], 1)

            walk(pe, step)

            for name, count in (("tanh_done", B), ("h_copied", B), ("val_done", B), ("logits_copied", B),
                                ("q_lo", NU * B), ("max_done", NU * B), ("exp_done", NU * B), ("ctxT_copied", B),
                                ("ffn_ready", 2), ("w2_params", 16)):
                pe.wait_ge(s[name], count)

            def up(n, g, e, half_):
                z = z2T[:, bass.ts(g, TB), :, :]
                cols = slice(e * I, (e + 1) * I)
                for first, hi, lo, read, done in ((0, w1_hi, w1_lo, "silu_done", "h1_psum"),
                                                  (2, w3_hi, w3_lo, "inner_done", "h3_psum")):
                    if not isinstance(n, int) or n >= 2:
                        pe.wait_ge(s[read], n - 1)
                    split_product(banks[first + half_][:, 0:TB * P],
                                  lambda tile, low: (lo if low else hi)[:, tile, cols],
                                  lambda tile, low: z[:, :, tile, :]).then_inc(s[done], 1)

            def down(n, e, half_):
                pe.wait_ge(s["inner_done"], n + 1)
                if not isinstance(n, int) or n >= 2:
                    pe.wait_ge(s["acc_done"], n - 1)
                for b in range(TB):
                    y = banks[4 + 2 * half_ + b // 2][0:P, (b % 2) * 256:(b % 2) * 256 + D]
                    last = mm(y, inner[:, half_, b * P:(b + 1) * P], w2_s[:, e, :])
                last.then_inc(s["y_psum"], 1)

            order = [E] + list(range(E))

            def two_groups(q):
                for m in range(2 * NE):
                    n = 2 * NE * q + m
                    if m + 1 < 2 * NE:
                        up(n + 1, 2 * q + (m + 1) // NE, order[(m + 1) % NE], (m + 1) % 2)
                    elif not (isinstance(q, int) and q == NG // 2 - 1):
                        up(n + 1, 2 * q + 2, order[0], 0)
                    down(n, order[m % NE], m % 2)

            up(0, 0, order[0], 0)
            two_groups(0)
            with pe.Fori(1, NG // 2 - 1) as q:
                two_groups(q)
            two_groups(NG // 2 - 1)


def kernel(**inputs):
    import concourse.bacc as bacc
    from concourse.bass_utils import run_bass_kernel_spmd

    v = {n: np.asarray(a) for n, a in inputs.items()}
    f32 = np.float32

    def two_tiles(w, bias):
        t = np.zeros((128, 2, D), f32)
        t[:, 0] = w.T[0:128]
        t[128 - CUT:127, 1] = w.T[128:D]
        t[127, 1] = bias
        return t

    def three_tiles(w):
        t = w.T
        return np.stack([t[0:128], np.concatenate([t[128:D], t[0:R]]), t[R:D]], 1)

    last_row = np.zeros((32, D), f32)
    last_row[31] = v["L0_tok_b"]
    basis = three_tiles(v["L0_attn_basis_w"])
    heads = v["L0_attn_head_residual"].transpose(1, 0, 2)
    w1 = np.concatenate([v["L0_ffn_w1"].reshape(E * I, D), v["L0_ffn_sw1"]])
    w3 = np.concatenate([v["L0_ffn_w3"].reshape(E * I, D), v["L0_ffn_sw3"]])
    w2 = np.concatenate([v["L0_ffn_w2"], v["L0_ffn_sw2"][None]])
    shift = np.zeros((128, 128), f32)
    shift[np.arange(1, 128), np.arange(0, 127)] = 1.0
    laid = {
        "x": v["x"],
        "w_tok": two_tiles(v["L0_tok_W_w"], v["L0_tok_W_b"]),
        "b_tok": last_row,
        "v_tok": np.broadcast_to(v["L0_tok_V_w"], (128, D)),
        "vb_tok": np.broadcast_to(v["L0_tok_V_b"], (128, 1)),
        "p_tok": two_tiles(v["L0_tok_P_w"], v["L0_tok_P_b"]),
        "attn_w": np.concatenate([basis, basis, three_tiles(v["L0_attn_value_w"])], 2),
        "attn_vb": np.broadcast_to(v["L0_attn_value_b"], (128, D)),
        "core": np.tile(v["L0_attn_core"], (2, 2)),
        "head_res": np.tile(heads, (2, 1, 2)),
        "gate_w": three_tiles(v["L0_ffn_gate_weight"]),
        "gate_b": np.broadcast_to(v["L0_ffn_gate_bias"], (128, E)),
        "w1": three_tiles(w1).reshape(128, 3 * NE * I),
        "w3": three_tiles(w3).reshape(128, 3 * NE * I),
        "w2": w2.transpose(2, 0, 1),
        "eye": np.eye(128, dtype=f32),
        "shift": shift,
    }
    nc = bacc.Bacc("TRN2", target_bir_lowering=False, num_devices=1)
    arrays, args = {}, []
    for name, a in laid.items():
        a = np.ascontiguousarray(a)
        arrays[f"in_{name}"] = a
        args.append(nc.dram_tensor(f"in_{name}", a.shape, mybir.dt.from_np(a.dtype), kind="ExternalInput").ap())
    args.append(nc.dram_tensor("out", (B, P, D), F32, kind="ExternalOutput").ap())
    audio_tower(nc, *args)
    result = run_bass_kernel_spmd(nc, [arrays], core_ids=[0])
    return result.results[0]["out"]
```

```python
import numpy as np
import concourse.bass as bass
from concourse import mybir
from contextlib import ExitStack

F32 = mybir.dt.float32
F16 = mybir.dt.float16
I32 = mybir.dt.int32
ALU = mybir.AluOpType
ACT = mybir.ActivationFunctionType
AX = mybir.AxisListType

B, S, D = 64, 256, 192
PL, STRIDE = 4, 2
P = (S - PL) // STRIDE + 1
NH, R = 12, 64
HD = D // NH
HV = HD + 1
U = 4
NU = NH // U
UW = U * P
E, TOPK, G = 8, 2, 4
I = 128
NE = E + 1
CUT = D + 1 - 128
SHIFT = 2.0 ** 15
TB = 4
NG = B // TB
LAST = B + 6
HEAD, TAIL = 8, B


def on(n):
    return not isinstance(n, int) or 0 <= n < B


def later(n, k):
    return not isinstance(n, int) or n >= k


def it_first(it, first):
    return isinstance(it, int) and it == first


def walk(eng, step):
    for it in range(HEAD):
        step(it, it % 2)
    with eng.Fori(HEAD // 2, TAIL // 2) as pair:
        for odd in range(2):
            step(2 * pair + odd, odd)
    for it in range(TAIL, LAST):
        step(it, it % 2)


def windows(x):
    return bass.AP(tensor=x.tensor, offset=0, ap=[[S * D, B], [STRIDE * D, P], [1, PL * D]])


def audio_tower(nc, x, w_tok, b_tok, v_tok, vb_tok, p_tok, attn_w, attn_vb, core, head_res,
                gate_w, gate_b, w1, w3, w2, eye, shift, out):
    with ExitStack() as ctx:
        def sb(name, shape, dt=F32):
            return ctx.enter_context(nc.sbuf_tensor(name, shape, dt))

        def bank(name, n=1):
            return ctx.enter_context(nc.psum_tensor(name, [128, n * 512], F32))

        def sem(name):
            return ctx.enter_context(nc.semaphore(name))

        w_tok_s = sb("w_tok_s", [128, 2, D])
        v_tok_s = sb("v_tok_s", [128, D])
        vb_s = sb("vb_s", [128, 1])
        p_tok_s = sb("p_tok_s", [128, 2, D])
        value_b = sb("value_b", [128, D])
        gate_bias = sb("gate_bias", [128, E])
        eye_s = sb("eye_s", [128, 128])
        eye16 = sb("eye16", [128, 128], F16)
        shift_s = sb("shift_s", [128, 128])
        AW = 128 + D
        attn_hi = sb("attn_hi", [128, 3, AW], F16)
        attn_lo = sb("attn_lo", [128, 2, AW], F16)
        gate_hi = sb("gate_hi", [128, 3, E], F16)
        gate_lo = sb("gate_lo", [128, 2, E], F16)
        w1_hi = sb("w1_hi", [128, 3, NE * I], F16)
        w1_lo = sb("w1_lo", [128, 2, NE * I], F16)
        w3_hi = sb("w3_hi", [128, 3, NE * I], F16)
        w3_lo = sb("w3_lo", [128, 2, NE * I], F16)
        w2_hi = sb("w2_hi", [128, NE, D], F16)
        w2_lo = sb("w2_lo", [128, NE, D], F16)
        head_hi = sb("head_hi", [128, NH, 128], F16)
        head_lo = sb("head_lo", [128, NH, 128], F16)
        stage = sb("stage", [128, 3 * NE * I])
        gate_raw = sb("gate_raw", [128, 3, E])
        head_raw = stage[:, 0:NH * 128].rearrange("p (h s) -> p h s", h=NH)
        core_raw = stage[:, NH * 128:NH * 128 + 128]
        b_tok_s = stage[:, NH * 128 + 256:NH * 128 + 256 + D]
        head_sum = stage[:, NH * 128 + 128:NH * 128 + 256]
        w2_raw = stage[:, 0:NE * D].rearrange("p (e d) -> p e d", e=NE)
        NSC = 7
        BASIS, VALUE, GATE, HEADS, W1, W3, W2 = range(NSC)
        amax = sb("amax", [128, NSC])
        amax_all = sb("amax_all", [128, NSC])
        power = sb("power", [128, NSC])
        inverse = sb("inverse", [128, NSC])
        exp_scale = sb("exp_scale", [128, 1])
        gate_scale = sb("gate_scale", [128, 1])
        inner_scale = sb("inner_scale", [128, 1])
        down_scale = sb("down_scale", [128, 1])
        eps = sb("eps", [128, 1])
        minus_half = sb("minus_half", [128, 1])
        zero = sb("zero", [128, 1])
        unshift = sb("unshift", [128, 1])

        pairs = sb("pairs", [128, 2, 2, D + 1])
        wins = sb("wins", [P, 2, PL, D])
        xT = sb("xT", [128, 2, 4 * 128])
        th = sb("th", [128, 2, 2 * D])
        score = sb("score", [128, 2, 2])
        win_max = sb("win_max", [P, 1])
        win_d = sb("win_d", [P, PL])
        win_e = sb("win_e", [P, PL])
        win_z = sb("win_z", [P, 1])
        win_r = sb("win_r", [P, 1])
        win_w = sb("win_w", [P, 2, PL])
        half = sb("half", [P, 2, D])
        pooled = sb("pooled", [P, 2, D + 1])
        pooledT = sb("pooledT", [128, 2, 2 * P])
        res = sb("res", [P, B, D])
        stats = sb("stats", [P, 2, 6])
        mv = sb("mv", [P, 2, 2])
        after_stats = sb("after_stats", [P, 1])
        rstd = sb("rstd", [P, 2, 1])
        vpe = sb("vpe", [P, 2, 1])
        xn = sb("xn", [P, 2, D])
        z1 = sb("z1", [P, 2, 2 * D], F16)
        z2 = sb("z2", [P, 2, 2 * D], F16)
        z1T = sb("z1T", [128, 2, 3, P], F16)
        z2T = sb("z2T", [128, B, 3, P], F16)
        lat_a = sb("lat_a", [128, 2, P], F16)
        lat_b = sb("lat_b", [128, 2, P], F16)
        vals = sb("vals", [P, 2, NH, HV])
        q_a = sb("q_a", [128, 2, NH * P], F16)
        attn_raw = q_a[:].rearrange("p a n -> p (a n)").bitcast(F32)[:, 0:3 * AW].rearrange("p (a n) -> p a n", a=3)
        q_b = sb("q_b", [128, 2, NH * P], F16)
        row_max = sb("row_max", [P, 2, NH])
        neg_max = sb("neg_max", [P, NH])
        max_hl = sb("max_hl", [P, 2, 2 * NH], F16)
        max_hlT = sb("max_hlT", [2 * NH, 2, P], F16)
        probs = sb("probs", [P, 2, UW])
        ctxT = sb("ctxT", [128, 2, NU * P])
        recip = sb("recip", [P, NH])
        att = sb("att", [P, 2, D])
        logits = sb("logits", [P, B, E])
        choice = logits
        GW = TB * P
        over_a, over_b = (q[:].rearrange("p a n -> p (a n)") for q in (q_a, q_b))
        silu = over_a[:, 0:4 * GW].bitcast(F32).rearrange("p (a n) -> p a n", a=2)
        inner = over_b[:, 0:4 * GW].bitcast(F32).rearrange("p (a n) -> p a n", a=2)
        inner_hi = over_a[:, 4 * GW:6 * GW].rearrange("p (a n) -> p a n", a=2)
        inner_lo = over_b[:, 4 * GW:6 * GW].rearrange("p (a n) -> p a n", a=2)

        sizes = (("sig", E), ("biased", E), ("masked", E), ("rank", E), ("cmp", E),
                 ("group", G), ("group_rank", G), ("group_cmp", G), ("norm", 1))
        room, at = {}, 0
        for name, width in sizes:
            room[name] = stage[0:P, at:at + B * width].rearrange("p (b e) -> p b e", e=width)
            at += B * width
        sig, biased, masked, rank, comp = (room[n] for n in ("sig", "biased", "masked", "rank", "cmp"))
        group, group_rank, group_cmp, norm = (room[n] for n in ("group", "group_rank", "group_cmp", "norm"))

        tok_bank, pool_bank, lat_bank, turn_bank = (bank(n) for n in ("tok_b", "pool_b", "lat_b_", "turn_b"))
        q_bank, max_bank, s_bank, ctx_bank = (bank(n) for n in ("q_bank", "max_b", "s_bank", "ctx_b"))
        banks = [tok_bank, pool_bank, lat_bank, turn_bank, q_bank, max_bank, s_bank, ctx_bank]
        lat16 = lat_bank[:, :].bitcast(F16)
        turn16 = turn_bank[:, :].bitcast(F16)

        s = {n: sem(n) for n in (
            "tok_params", "attn_params", "head_params", "w1_params", "w3_params", "w2_params",
            "amax_part", "amax_done", "prep", "w_hi", "consts", "tok_ready", "attn_ready", "ffn_ready",
            "pairs_in", "wins_in", "max_rows_in",
            "xT_psum", "tok_psum", "win_psum", "pooledT_psum", "h_psum", "z1T_psum", "lat_psum",
            "val_psum", "q_psum", "max_psum", "s_psum", "ctx_psum", "maxT_psum", "att_psum",
            "z2T_psum", "logit_psum",
            "xT_copied", "tanh_done", "win_exp", "pooledT_copied", "h_copied", "lat_hi", "q_hi",
            "exp_done", "ctxT_copied", "z2T_copied",
            "score_part", "score_done", "win_max_done", "win_d_done", "win_z_done", "win_r_done",
            "win_w_done", "stats1", "mv1", "xn1", "stats2", "mv2", "xn2", "z1T_copied", "lat_lo",
            "val_done", "q_lo", "max_done", "maxT_copied", "recip_done", "att_done", "logits_copied",
            "vpe1", "rstd1", "z1_hi", "z1_done", "vpe2", "rstd2", "z2_hi", "z2_done", "lat_b_done",
            "prod_done", "half_done", "pooled_done", "neg_done", "max_hi", "max_hl_done", "res_done",
            "gate_tanh", "gate_step", "h1_psum", "h3_psum", "silu_done", "inner_done",
            "inner_hi_done", "inner_lo_done", "y_psum", "acc_done", "stored",
        )}

        block = ctx.enter_context(nc.Block())

        @block.sync
        def _(sp):
            for dst, src in ((w_tok_s[:], w_tok), (b_tok_s[96:128, :], b_tok), (v_tok_s[:], v_tok),
                             (vb_s[:], vb_tok), (p_tok_s[:], p_tok), (eye_s[:], eye), (shift_s[:], shift)):
                sp.dma_start(dst, src).then_inc(s["tok_params"], 16)
            for dst, src in ((attn_raw, attn_w), (value_b[:], attn_vb), (gate_raw[:], gate_w),
                             (gate_bias[:], gate_b)):
                sp.dma_start(dst, src).then_inc(s["attn_params"], 16)
            sp.dma_start(head_raw, head_res).then_inc(s["head_params"], 16)
            sp.dma_start(core_raw, core).then_inc(s["head_params"], 16)

            def step(it, par):
                n, w, j = it, it - 1, it - 4
                if on(w):
                    if later(w, 1):
                        sp.wait_ge(s["half_done"], w)
                    sp.dma_start(wins[:, 1 - par, :, :].rearrange("p l d -> p (l d)"),
                                 windows(x)[w, :, :]).then_inc(s["wins_in"], 16)
                if on(n):
                    if later(n, 1):
                        sp.wait_ge(s["xT_psum"], n)
                    sp.dma_start(pairs[:, par, :, 0:D],
                                 x[n, :, :].rearrange("(q c) d -> q c d", c=2)).then_inc(s["pairs_in"], 16)
                if on(j):
                    sp.wait_ge(s["maxT_copied"], j + 1)
                    sp.dma_start(q_b[R:R + 2, par, :].rearrange("r (h n) -> r h n", h=NH),
                                 max_hlT[:, par, :]).then_inc(s["max_rows_in"], 16)
                if isinstance(it, int) and it == 1:
                    sp.wait_ge(s["attn_ready"], 1)
                    sp.dma_start(stage[:], w1).then_inc(s["w1_params"], 16)
                if isinstance(it, int) and it == 3:
                    sp.wait_ge(s["ffn_ready"], 1)
                    sp.dma_start(stage[:], w3).then_inc(s["w3_params"], 16)
                if isinstance(it, int) and it == 5:
                    sp.wait_ge(s["ffn_ready"], 2)
                    sp.dma_start(w2_raw, w2).then_inc(s["w2_params"], 16)

            walk(sp, step)
            with sp.Fori(0, NG) as g:
                sp.wait_ge(s["acc_done"], E * (g + 1) + NG)
                sp.dma_start(out[bass.ts(g, TB), :, :].rearrange("b p d -> p b d"),
                             res[:, bass.ts(g, TB), :]).then_inc(s["stored"], 16)
            sp.wait_ge(s["stored"], 16 * NG)

        @block.gpsimd
        def _(pool):
            for m, (place, value) in enumerate((
                    (pairs[:, :, :, D:D + 1], 1.0), (pooled[:, :, D:D + 1], 1.0), (vals[:, :, :, HD:HV], 1.0),
                    (q_b[R:128, :, :], 0.0), (lat_b[R:128, :, :], 0.0), (lat_b[R:R + 2, :, :], SHIFT),
                    (eps[:], 1e-5), (minus_half[:], -0.5), (zero[:], 0.0), (unshift[:], -1.0 / SHIFT))):
                pool.memset(place, value).then_inc(s["consts"], 1)
                pool.wait_ge(s["consts"], m + 1)
            pool.wait_ge(s["amax_part"], 1)
            pool.partition_all_reduce(amax_all[:, 0:4], amax[:, 0:4], 128,
                                      bass.bass_isa.ReduceOp.absmax).then_inc(s["amax_done"], 1)

            def norm_scale(n, k, mv_done, vpe_done, rstd_done):
                pool.wait_ge(mv_done, n + 1)
                pool.tensor_tensor(vpe[:, k, :], mv[:, k, 1:2], eps[0:P, :], ALU.add).then_inc(vpe_done, 1)
                pool.wait_ge(vpe_done, n + 1)
                pool.tensor_tensor(rstd[:, k, :], vpe[:, k, :], minus_half[0:P, :],
                                   ALU.pow).then_inc(rstd_done, 1)

            def norm_lo(n, k, par, z, hi_done, lo_done):
                pool.wait_ge(hi_done, n + 1)
                pool.tensor_tensor(z[:, par, D:2 * D], xn[:, k, :], z[:, par, 0:D],
                                   ALU.subtract).then_inc(lo_done, 1)

            def step(it, par):
                t, a, z, j, k, l = (it - m for m in range(1, 7))
                odd = 1 - par
                if on(z):
                    norm_scale(z, 0, s["mv1"], s["vpe1"], s["rstd1"])
                if on(l):
                    norm_lo(l, 1, par, z2, s["z2_hi"], s["z2_done"])
                if on(z):
                    norm_lo(z, 0, odd, z1, s["z1_hi"], s["z1_done"])
                if on(a):
                    pool.wait_ge(s["win_w_done"], a + 1)
                    pool.wait_ge(s["wins_in"], 16 * (a + 1))
                    pool.tensor_tensor(wins[:, par, :, :], wins[:, par, :, :],
                                       win_w[:, par, :].unsqueeze(2).to_broadcast([P, PL, D]),
                                       ALU.mult).then_inc(s["prod_done"], 1)
                    pool.wait_ge(s["prod_done"], a + 1)
                    if later(a, 1):
                        pool.wait_ge(s["pooled_done"], a)
                    pool.tensor_tensor(half[:], wins[:, par, 0:2, :], wins[:, par, 2:4, :],
                                       ALU.add).then_inc(s["half_done"], 1)
                    pool.wait_ge(s["half_done"], a + 1)
                    if later(a, 2):
                        pool.wait_ge(s["pooledT_psum"], a - 1)
                    pool.tensor_tensor(pooled[:, par, 0:D], half[:, 0, :], half[:, 1, :],
                                       ALU.add).then_inc(s["pooled_done"], 1)
                if on(j):
                    pool.wait_ge(s["max_done"], NU * (j + 1))
                    pool.tensor_tensor(neg_max[:], row_max[:, par, :], unshift[0:P, :].to_broadcast([P, NH]),
                                       ALU.mult).then_inc(s["neg_done"], 1)
                    pool.wait_ge(s["neg_done"], j + 1)
                    if later(j, 2):
                        pool.wait_ge(s["maxT_psum"], j - 1)
                    pool.tensor_tensor(max_hl[:, par, 0:NH], neg_max[:], zero[0:P, :].to_broadcast([P, NH]),
                                       ALU.add).then_inc(s["max_hi"], 1)
                    pool.wait_ge(s["max_hi"], j + 1)
                    pool.tensor_tensor(max_hl[:, par, NH:2 * NH], neg_max[:], max_hl[:, par, 0:NH],
                                       ALU.subtract).then_inc(s["max_hl_done"], 1)
                if on(k):
                    pool.wait_ge(s["att_done"], k + 1)
                    pool.tensor_tensor(res[:, k, :], res[:, k, :], att[:, odd, :],
                                       ALU.add).then_inc(s["res_done"], 1)
                    norm_scale(k, 1, s["mv2"], s["vpe2"], s["rstd2"])
                if isinstance(it, int) and it in (1, 3, 5):
                    c = 4 + it // 2
                    pool.wait_ge(s["amax_part"], c - 2)
                    pool.partition_all_reduce(amax_all[:, c:c + 1], amax[:, c:c + 1], 128,
                                              bass.bass_isa.ReduceOp.absmax).then_inc(s["amax_done"], 1)

            walk(pool, step)

            def inner_los(n, half_):
                pool.wait_ge(s["inner_hi_done"], n + 1)
                if not isinstance(n, int) or n >= 2:
                    pool.wait_ge(s["y_psum"], n - 1)
                pool.tensor_tensor(inner_lo[:, half_, :], inner[:, half_, :], inner_hi[:, half_, :],
                                   ALU.subtract).then_inc(s["inner_lo_done"], 1)

            for m in range(2):
                inner_los(m, m)
            with pool.Fori(1, NE * NG // 2) as q:
                for m in range(2):
                    inner_los(2 * q + m, m)

        @block.scalar
        def _(act):
            def step(it, par):
                t, a, z, j, k, l = (it - m for m in range(1, 7))
                odd = 1 - par

                def query_hi(u):
                    if not on(j):
                        return
                    act.wait_ge(s["q_psum"], NU * j + u + 1)
                    act.activation(q_a[:, par, u * UW:(u + 1) * UW], q_bank[:, 0:UW],
                                   ACT.Copy).then_inc(s["q_hi"], 1)

                def norm_hi(n, k, half_, z, xn_done, hi_done, readers):
                    act.wait_ge(xn_done, n + 1)
                    if later(n, 2):
                        act.wait_ge(readers, n - 1)
                    act.activation(z[:, half_, 0:D], xn[:, k, :], ACT.Copy).then_inc(hi_done, 1)

                def exps(u):
                    if not on(k):
                        return
                    act.wait_ge(s["s_psum"], NU * k + u + 1)
                    if later(k, 1) or u >= 2:
                        act.wait_ge(s["ctx_psum"], NU * k + u - 1)
                    act.activation(probs[:, (odd + u) % 2, :], s_bank[0:P, 0:UW], ACT.Exp,
                                   scale=exp_scale[0:P, :]).then_inc(s["exp_done"], 1)

                if on(t):
                    act.wait_ge(s["xT_psum"], t + 1)
                    if later(t, 2):
                        act.wait_ge(s["tok_psum"], t - 1)
                    act.activation(xT[:, odd, :], tok_bank[:, :], ACT.Copy).then_inc(s["xT_copied"], 1)
                query_hi(0)
                if on(l):
                    norm_hi(l, 1, par, z2, s["xn2"], s["z2_hi"], s["z2T_psum"])
                if it_first(it, 5):
                    act.wait_ge(s["attn_ready"], 1)
                exps(0)
                if on(a):
                    act.wait_ge(s["win_d_done"], a + 1)
                    act.activation(win_e[:], win_d[:], ACT.Exp).then_inc(s["win_exp"], 1)
                if on(z):
                    norm_hi(z, 0, odd, z1, s["xn1"], s["z1_hi"], s["z1T_psum"])
                query_hi(1)
                exps(1)
                if on(l):
                    act.wait_ge(s["z2T_psum"], l + 1)
                    act.activation(z2T[:, l, :, :], turn16[:, 0:384].rearrange("p (c n) -> p c n", c=3)[:, :, 0:P],
                                   ACT.Copy).then_inc(s["z2T_copied"], 1)
                if on(z):
                    act.wait_ge(s["z1T_psum"], z + 1)
                    act.activation(z1T[:, odd, :, :], lat16[:, 0:384].rearrange("p (c n) -> p c n", c=3)[:, :, 0:P],
                                   ACT.Copy).then_inc(s["z1T_copied"], 1)
                query_hi(2)
                exps(2)
                if on(z):
                    act.wait_ge(s["lat_psum"], z + 1)
                    if later(z, 2):
                        act.wait_ge(s["s_psum"], NU * (z - 1))
                    act.activation(lat_a[:, odd, :], lat_bank[:, 0:P], ACT.Copy).then_inc(s["lat_hi"], 1)
                    act.activation(lat_b[0:R, odd, :], lat_bank[0:R, 0:P], ACT.Copy).then_inc(s["lat_b_done"], 1)
                if on(l):
                    act.wait_ge(s["logit_psum"], l + 1)
                    act.activation(logits[:, l, :], turn_bank[0:P, 0:E], ACT.Copy).then_inc(s["logits_copied"], 1)
                if on(k):
                    act.wait_ge(s["ctx_psum"], NU * (k + 1))
                    if later(k, 2):
                        act.wait_ge(s["att_psum"], k - 1)
                    act.activation(ctxT[:, odd, :], ctx_bank[:, 0:NU * P],
                                   ACT.Copy).then_inc(s["ctxT_copied"], 1)
                if on(t):
                    act.wait_ge(s["tok_psum"], t + 1)
                    if later(t, 2):
                        act.wait_ge(s["score_done"], t - 1)
                    act.activation(th[:, odd, :], tok_bank[:, 0:2 * D], ACT.Tanh).then_inc(s["tanh_done"], 1)
                if on(a):
                    act.wait_ge(s["pooledT_psum"], a + 1)
                    if later(a, 2):
                        act.wait_ge(s["h_psum"], a - 1)
                    act.activation(pooledT[:, par, :], pool_bank[:, 0:2 * P],
                                   ACT.Copy).then_inc(s["pooledT_copied"], 1)
                if on(j):
                    act.wait_ge(s["maxT_psum"], j + 1)
                    if later(j, 2):
                        act.wait_ge(s["max_rows_in"], 16 * (j - 1))
                    act.activation(max_hlT[:, par, :], lat16[0:2 * NH, 0:P], ACT.Copy).then_inc(s["maxT_copied"], 1)
                if on(a):
                    act.wait_ge(s["h_psum"], a + 1)
                    act.activation(res[:, a, :], pool_bank[0:P, 0:D], ACT.Copy).then_inc(s["h_copied"], 1)
            walk(act, step)
            act.wait_ge(s["logits_copied"], B)
            act.activation(logits[:], logits[:], ACT.Tanh, scale=gate_scale[0:P, :]).then_inc(s["gate_tanh"], 1)

            def silus(n, half_):
                act.wait_ge(s["h1_psum"], n + 1)
                if not isinstance(n, int) or n >= 2:
                    act.wait_ge(s["inner_done"], n - 1)
                act.activation(silu[:, half_, :], banks[half_][:, 0:TB * P], ACT.Silu,
                               scale=power[:, W1:W1 + 1]).then_inc(s["silu_done"], 1)

            def inner_his(n, half_):
                act.wait_ge(s["inner_done"], n + 1)
                if not isinstance(n, int) or n >= 2:
                    act.wait_ge(s["y_psum"], n - 1)
                act.activation(inner_hi[:, half_, :], inner[:, half_, :], ACT.Copy).then_inc(s["inner_hi_done"], 1)

            for m in range(2):
                silus(m, m)
                inner_his(m, m)
            with act.Fori(1, NE * NG // 2) as q:
                for m in range(2):
                    silus(2 * q + m, m)
                    inner_his(2 * q + m, m)

        @block.vector
        def _(dve):
            prepared = [0]

            def link(ins):
                prepared[0] += 1
                ins.then_inc(s["prep"], 1)
                dve.wait_ge(s["prep"], prepared[0])

            def scale_of(c0, c1):
                link(dve.tensor_scalar(amax_all[:, c0:c1], amax_all[:, c0:c1], 2.0 ** -100, None, ALU.max))
                link(dve.tensor_scalar(power[:, c0:c1].bitcast(I32), amax_all[:, c0:c1].bitcast(I32),
                                       0x7F800000, None, ALU.bitwise_and))
                link(dve.reciprocal(inverse[:, c0:c1], power[:, c0:c1]))

            def split(hi, lo, raw, lo_raw, hi_part, c):
                link(dve.tensor_scalar(hi, raw, inverse[:, c:c + 1], None, ALU.mult))
                link(dve.scalar_tensor_tensor(lo, lo_raw, inverse[:, c:c + 1], hi_part, ALU.mult, ALU.subtract))

            link(dve.memset(ctx_bank[:, :], 0.0))
            dve.wait_ge(s["tok_params"], 16 * 7)
            link(dve.tensor_copy(eye16[:], eye_s[:]))
            dve.tensor_tensor(w_tok_s[96:128, 1, :], w_tok_s[96:128, 1, :], b_tok_s[96:128, :],
                              ALU.add).then_inc(s["tok_ready"], 1)

            dve.wait_ge(s["attn_params"], 16 * 4)
            dve.wait_ge(s["head_params"], 16 * 2)
            link(dve.tensor_reduce(head_sum, head_raw.rearrange("p h s -> p s h"), AX.X, ALU.add))
            link(dve.tensor_tensor(core_raw, core_raw, head_sum, ALU.subtract))
            link(dve.tensor_scalar(core_raw, core_raw, 1.0 / NH, None, ALU.mult))
            link(dve.tensor_tensor(head_raw, head_raw, core_raw.unsqueeze(1).to_broadcast([128, NH, 128]), ALU.add))

            def biggest(c, src, axis):
                return dve.tensor_reduce(amax[:, c:c + 1], src, axis, ALU.max, apply_absolute_value=True)

            link(biggest(BASIS, attn_raw[:, 0:2, 0:128], AX.XY))
            link(biggest(VALUE, attn_raw[:, 0:2, 128:AW], AX.XY))
            link(biggest(GATE, gate_raw[:, 0:2, :], AX.XY))
            biggest(HEADS, head_raw, AX.XY).then_inc(s["amax_part"], 1)
            dve.wait_ge(s["amax_done"], 1)
            scale_of(0, 4)
            split(attn_hi[:, :, 0:128], attn_lo[:, :, 0:128], attn_raw[:, :, 0:128],
                  attn_raw[:, 0:2, 0:128], attn_hi[:, 0:2, 0:128], BASIS)
            split(attn_hi[:, :, 128:AW], attn_lo[:, :, 128:AW], attn_raw[:, :, 128:AW],
                  attn_raw[:, 0:2, 128:AW], attn_hi[:, 0:2, 128:AW], VALUE)
            split(gate_hi[:], gate_lo[:], gate_raw[:], gate_raw[:, 0:2, :], gate_hi[:, 0:2, :], GATE)
            split(head_hi[:], head_lo[:], head_raw, head_raw, head_hi[:], HEADS)
            link(dve.tensor_tensor(exp_scale[:], power[:, BASIS:BASIS + 1], power[:, BASIS:BASIS + 1], ALU.mult))
            link(dve.tensor_tensor(exp_scale[:], exp_scale[:], power[:, HEADS:HEADS + 1], ALU.mult))
            link(dve.tensor_scalar(exp_scale[:], exp_scale[:], R ** -0.5, None, ALU.mult))
            dve.tensor_scalar(gate_scale[:], power[:, GATE:GATE + 1], 0.5, None,
                              ALU.mult).then_inc(s["attn_ready"], 1)

            def prepare_ffn(c, params, hi, lo):
                dve.wait_ge(params, 16)
                raw = stage[:].rearrange("p (a n) -> p a n", a=3)
                biggest(c, raw[:, 0:2, :], AX.XY).then_inc(s["amax_part"], 1)
                dve.wait_ge(s["amax_done"], c - 2)
                scale_of(c, c + 1)
                for tile in range(3):
                    dve.tensor_scalar(hi[:, tile, :], raw[:, tile, :], inverse[:, c:c + 1], None,
                                      ALU.mult).then_inc(s["w_hi"], 1)
                    dve.wait_ge(s["w_hi"], 3 * (c - W1) + tile + 1)
                for tile in range(2):
                    last = dve.scalar_tensor_tensor(lo[:, tile, :], raw[:, tile, :], inverse[:, c:c + 1],
                                                    hi[:, tile, :], ALU.mult, ALU.subtract)
                last.then_inc(s["ffn_ready"], 1)

            def prepare_w2():
                dve.wait_ge(s["w2_params"], 16)
                biggest(W2, w2_raw, AX.XY).then_inc(s["amax_part"], 1)
                dve.wait_ge(s["amax_done"], W2 - 2)
                scale_of(W2, W2 + 1)
                link(dve.tensor_scalar(inner_scale[:], inverse[:, W1:W1 + 1], 0.25, None, ALU.mult))
                link(dve.tensor_tensor(down_scale[:], power[:, W1:W1 + 1], power[:, W3:W3 + 1], ALU.mult))
                link(dve.tensor_tensor(down_scale[:], down_scale[:], power[:, W2:W2 + 1], ALU.mult))
                link(dve.tensor_scalar(down_scale[:], down_scale[:], 4.0, None, ALU.mult))
                link(dve.tensor_scalar(w2_hi[:], w2_raw, inverse[:, W2:W2 + 1], None, ALU.mult))
                dve.scalar_tensor_tensor(w2_lo[:], w2_raw, inverse[:, W2:W2 + 1], w2_hi[:],
                                         ALU.mult, ALU.subtract).then_inc(s["ffn_ready"], 1)

            def norm_stats(n, k, stats_done):
                dve.bn_stats(stats[:, k, :], res[:, n, :]).then_inc(stats_done, 1)
                dve.wait_ge(stats_done, n + 1)
                dve.memset(after_stats[:], 0.0)

            def norm_mean(k, mv_done):
                dve.bn_aggr(mv[:, k, :], stats[:, k, :]).then_inc(mv_done, 1)

            def normed(n, k, rstd_done, xn_done, split_done):
                dve.wait_ge(rstd_done, n + 1)
                if later(n, 1):
                    dve.wait_ge(split_done, n)
                dve.tensor_scalar(xn[:, k, :], res[:, n, :], mv[:, k, 0:1], rstd[:, k, :],
                                  ALU.subtract, ALU.mult).then_inc(xn_done, 1)

            def step(it, par):
                t, a, z, j, k, l = (it - m for m in range(1, 7))
                odd = 1 - par

                def query_lo(u):
                    if not on(j):
                        return
                    dve.wait_ge(s["q_hi"], NU * j + u + 1)
                    dve.tensor_tensor(q_b[0:R, par, u * UW:(u + 1) * UW], q_bank[0:R, 0:UW],
                                      q_a[0:R, par, u * UW:(u + 1) * UW], ALU.subtract).then_inc(s["q_lo"], 1)

                def maxima(u):
                    if not on(j):
                        return
                    dve.wait_ge(s["max_psum"], NU * j + u + 1)
                    if u == 0 and later(j, 2):
                        dve.wait_ge(s["neg_done"], j - 1)
                    dve.tensor_reduce(row_max[:, par, u * U:(u + 1) * U],
                                      max_bank[0:P, 0:UW].rearrange("p (h m) -> p h m", h=U),
                                      AX.X, ALU.max).then_inc(s["max_done"], 1)

                if on(z):
                    dve.wait_ge(s["h_copied"], z + 1)
                    norm_stats(z, 0, s["stats1"])
                    norm_mean(0, s["mv1"])
                query_lo(0)
                if on(l):
                    normed(l, 1, s["rstd2"], s["xn2"], s["z2_done"])
                if on(a):
                    dve.wait_ge(s["win_psum"], a + 1)
                    dve.tensor_reduce(win_max[:], pool_bank[0:P, 0:PL], AX.X, ALU.max).then_inc(s["win_max_done"], 1)
                    dve.wait_ge(s["win_max_done"], a + 1)
                    dve.tensor_scalar(win_d[:], pool_bank[0:P, 0:PL], win_max[:], None,
                                      ALU.subtract).then_inc(s["win_d_done"], 1)
                if on(z):
                    normed(z, 0, s["rstd1"], s["xn1"], s["z1_done"])
                maxima(0)
                if on(a):
                    dve.wait_ge(s["win_exp"], a + 1)
                    dve.tensor_reduce(win_z[:], win_e[:], AX.X, ALU.add).then_inc(s["win_z_done"], 1)
                    dve.wait_ge(s["win_z_done"], a + 1)
                    dve.reciprocal(win_r[:], win_z[:]).then_inc(s["win_r_done"], 1)
                    dve.wait_ge(s["win_r_done"], a + 1)
                    if later(a, 2):
                        dve.wait_ge(s["prod_done"], a - 1)
                    dve.tensor_scalar(win_w[:, par, :], win_e[:], win_r[:], None,
                                      ALU.mult).then_inc(s["win_w_done"], 1)
                query_lo(1)
                maxima(1)
                query_lo(2)
                maxima(2)
                if on(z):
                    dve.wait_ge(s["lat_b_done"], z + 1)
                    dve.tensor_tensor(lat_a[R:128, odd, :], lat_bank[R:128, 0:P], lat_a[R:128, odd, :],
                                      ALU.subtract).then_inc(s["lat_lo"], 1)
                if on(k):
                    dve.wait_ge(s["att_psum"], k + 1)
                    att_ps = turn_bank[0:P, 0:NU * 128].rearrange("p (h d) -> p h d", d=32)
                    dve.reciprocal(recip[:], att_ps[:, :, HD]).then_inc(s["recip_done"], 1)
                    dve.wait_ge(s["recip_done"], k + 1)
                    if later(k, 2):
                        dve.wait_ge(s["res_done"], k - 1)
                    dve.tensor_tensor(att[:, odd, :].rearrange("p (h d) -> p h d", d=HD), att_ps[:, :, 0:HD],
                                      recip[:].unsqueeze(2).to_broadcast([P, NH, HD]),
                                      ALU.mult).then_inc(s["att_done"], 1)
                if on(z):
                    dve.wait_ge(s["val_psum"], z + 1)
                    dve.scalar_tensor_tensor(
                        vals[:, odd, :, 0:HD], max_bank[0:P, 0:D].rearrange("p (h d) -> p h d", d=HD),
                        power[0:P, VALUE:VALUE + 1], value_b[0:P, :].rearrange("p (h d) -> p h d", d=HD),
                        ALU.mult, ALU.add).then_inc(s["val_done"], 1)
                if on(t):
                    dve.wait_ge(s["tanh_done"], t + 1)
                    if later(t, 2):
                        dve.wait_ge(s["win_psum"], t - 1)
                    for c in range(2):
                        dve.tensor_tensor_reduce(
                            out=th[:, odd, c * D:(c + 1) * D], in0=th[:, odd, c * D:(c + 1) * D], in1=v_tok_s[:], scale=1.0,
                            scalar=vb_s[:, 0:1], op0=ALU.mult, op1=ALU.add,
                            accum_out=score[:, odd, c:c + 1]).then_inc(s["score_part" if c == 0 else "score_done"], 1)
                        if c == 0:
                            dve.wait_ge(s["score_part"], t + 1)
                if on(k):
                    dve.wait_ge(s["res_done"], k + 1)
                    norm_stats(k, 1, s["stats2"])
                    norm_mean(1, s["mv2"])
                if isinstance(it, int) and it == 1:
                    prepare_ffn(W1, s["w1_params"], w1_hi, w1_lo)
                if isinstance(it, int) and it == 3:
                    prepare_ffn(W3, s["w3_params"], w3_hi, w3_lo)
                if isinstance(it, int) and it == 5:
                    prepare_w2()

            walk(dve, step)

            def inners(n, half_):
                dve.wait_ge(s["silu_done"], n + 1)
                dve.wait_ge(s["h3_psum"], n + 1)
                dve.scalar_tensor_tensor(inner[:, half_, :], banks[2 + half_][:, 0:GW], inner_scale[:],
                                         silu[:, half_, :], ALU.mult, ALU.mult).then_inc(s["inner_done"], 1)

            def accumulate(n, g, e, half_):
                dve.wait_ge(s["y_psum"], n + 1)
                if not isinstance(n, int) or n >= 1:
                    dve.wait_ge(s["acc_done"], n)
                for b in range(TB):
                    y = banks[4 + 2 * half_ + b // 2][0:P, (b % 2) * 256:(b % 2) * 256 + D]
                    r = res[:, TB * g + b, :]
                    weight = down_scale[0:P, :] if e == E else choice[:, TB * g + b, e:e + 1]
                    ins = dve.scalar_tensor_tensor(r, y, weight, r, ALU.mult, ALU.add)
                ins.then_inc(s["acc_done"], 1)

            steps = [0]

            def then(ins):
                steps[0] += 1
                ins.then_inc(s["gate_step"], 1)
                dve.wait_ge(s["gate_step"], steps[0])

            def first_ranks(out_, n):
                for e in range(n):
                    then(dve.memset(out_[:, :, e:e + 1], float(n - 1 - e)))

            def compare(out_, val, tmp, n, d):
                then(dve.tensor_tensor(tmp[:, :, 0:n - d], val[:, :, 0:n - d], val[:, :, d:n], ALU.is_ge))
                then(dve.tensor_tensor(out_[:, :, d:n], out_[:, :, d:n], tmp[:, :, 0:n - d], ALU.add))
                then(dve.tensor_tensor(out_[:, :, 0:n - d], out_[:, :, 0:n - d], tmp[:, :, 0:n - d], ALU.subtract))

            def of_group(values):
                return (values.rearrange("p b g -> p (b g)").unsqueeze(2).to_broadcast([P, B * G, E // G]))

            def gate_part(m):
                pair = biased.rearrange("p b (g e) -> p b g e", e=E // G)
                in_pairs = masked.rearrange("p b (g e) -> p (b g) e", e=E // G)
                if m == 0:
                    dve.wait_ge(s["gate_tanh"], 1)
                    then(dve.tensor_scalar(sig, logits[:], 0.5, 0.5, ALU.mult, ALU.add))
                    then(dve.tensor_tensor(biased, sig, gate_bias[0:P, :].unsqueeze(1).to_broadcast([P, B, E]),
                                           ALU.add))
                elif m == 1:
                    then(dve.tensor_tensor(group, pair[:, :, :, 0], pair[:, :, :, 1], ALU.add))
                    first_ranks(group_rank, G)
                elif m == 2:
                    compare(group_rank, group, group_cmp, G, 1)
                    compare(group_rank, group, group_cmp, G, 2)
                elif m == 3:
                    compare(group_rank, group, group_cmp, G, 3)
                    then(dve.tensor_scalar(group_cmp, group_rank, 1.5, None, ALU.is_lt))
                elif m == 4:
                    then(dve.tensor_scalar(group, group_cmp, 1e30, -1e30, ALU.mult, ALU.add))
                    then(dve.tensor_tensor(in_pairs, biased.rearrange("p b (g e) -> p (b g) e", e=E // G),
                                           of_group(group_cmp), ALU.mult))
                elif m == 5:
                    then(dve.tensor_tensor(in_pairs, in_pairs, of_group(group), ALU.add))
                    first_ranks(rank, E)
                elif m < 5 + E:
                    compare(rank, masked, comp, E, m - 5)
                elif m == 5 + E:
                    then(dve.scalar_tensor_tensor(masked, rank, TOPK - 0.5, sig, ALU.is_lt, ALU.mult))
                    then(dve.tensor_reduce(norm[:, :, 0], masked, AX.X, ALU.add))
                elif m == 6 + E:
                    then(dve.tensor_scalar(norm, norm, 1e-6, None, ALU.add))
                    then(dve.reciprocal(norm, norm))
                    then(dve.tensor_scalar(norm, norm, down_scale[0:P, :], None, ALU.mult))
                else:
                    then(dve.tensor_tensor(choice[:], masked, norm.to_broadcast([P, B, E]), ALU.mult))

            inners(0, 0)
            for n in range(NG):
                inners(n + 1, (n + 1) % 2)
                accumulate(n, n, E, n % 2)
                gate_part(n)

            def experts(g, last=False):
                for e in range(E):
                    n = NG + E * g + e
                    if not (last and e == E - 1):
                        inners(n + 1, 1 - e % 2)
                    accumulate(n, g, e, e % 2)

            with dve.Fori(0, NG - 1) as g:
                experts(g)
            experts(NG - 1, last=True)

        @block.tensor
        def _(pe):
            def mm(out_, lhsT, rhs, start=True, stop=True):
                return pe.matmul(out_, lhsT, rhs, start=start, stop=stop)

            def split_product(out_, left, right):
                terms = [(0, 0), (1, 0), (2, 0), (0, 1), (1, 1)]
                for m, (tile, lo) in enumerate(terms):
                    last = mm(out_, left(tile, lo), right(tile, lo), start=(m == 0), stop=(m == len(terms) - 1))
                return last

            def norm_transposes(dst16, z, par):
                for c in range(3):
                    last = pe.transpose(dst16[:, c * 128:c * 128 + P], z[:, par, c * 128:(c + 1) * 128],
                                        eye16[0:P, 0:P])
                return last

            def step(it, par):
                t, a, z, j, k, l = (it - m for m in range(1, 7))
                odd = 1 - par

                def queries(u):
                    if not on(j):
                        return
                    if u == 0:
                        pe.wait_ge(s["lat_lo"], j + 1)
                    if later(j, 1) or u:
                        pe.wait_ge(s["q_lo"], NU * j + u)
                    for h in range(U):
                        o = q_bank[:, h * P:(h + 1) * P]
                        mm(o, head_hi[:, u * U + h, :], lat_a[:, par, :], stop=False)
                        last = mm(o, head_lo[:, u * U + h, :], lat_a[:, par, :], start=False)
                    last.then_inc(s["q_psum"], 1)

                def max_scores(u):
                    if not on(j):
                        return
                    pe.wait_ge(s["q_hi"], NU * j + u + 1)
                    if u == 0:
                        pe.wait_ge(s["val_done"], j + 1)
                    else:
                        pe.wait_ge(s["max_done"], NU * j + u)
                    for h in range(U):
                        c = (u * U + h) * P
                        last = mm(max_bank[0:P, h * P:(h + 1) * P], q_a[:, par, c:c + P], lat_a[:, par, :])
                    last.then_inc(s["max_psum"], 1)

                def scores(u):
                    if not on(k):
                        return
                    if u == 0:
                        pe.wait_ge(s["max_rows_in"], 16 * (k + 1))
                        pe.wait_ge(s["lat_b_done"], k + 1)
                        pe.wait_ge(s["q_lo"], NU * (k + 1))
                    if later(k, 1) or u:
                        pe.wait_ge(s["exp_done"], NU * k + u)
                    cols = slice(u * UW, (u + 1) * UW)
                    mm(s_bank[0:P, 0:UW], lat_a[:, odd, :], q_a[:, odd, cols], stop=False)
                    mm(s_bank[0:P, 0:UW], lat_b[:, odd, :], q_b[:, odd, cols],
                       start=False).then_inc(s["s_psum"], 1)

                def token_layer(c):
                    if not on(t):
                        return
                    pe.wait_ge(s["xT_copied"], t + 1)
                    for tile in range(2):
                        o = (2 * c + tile) * 128
                        last = mm(tok_bank[:, c * D:(c + 1) * D], xT[:, odd, o:o + 128], w_tok_s[:, tile, :],
                                  start=(tile == 0), stop=(tile == 1))
                    if c == 1:
                        last.then_inc(s["tok_psum"], 1)

                def weighted(u):
                    if not on(k):
                        return
                    pe.wait_ge(s["exp_done"], NU * k + u + 1)
                    if u == 0 and later(k, 1):
                        pe.wait_ge(s["ctxT_copied"], k)
                    for h in range(U):
                        last = pe.matmul(ctx_bank[32 * h:32 * h + HV, u * P:(u + 1) * P],
                                         vals[:, odd, u * U + h, :], probs[:, (odd + u) % 2, h * P:(h + 1) * P],
                                         start=True, stop=True, tile_position=(0, 32 * h))
                    last.then_inc(s["ctx_psum"], 1)

                if on(t):
                    if it_first(it, 1):
                        pe.wait_ge(s["consts"], 10)
                        pe.wait_ge(s["tok_ready"], 1)
                    pe.wait_ge(s["pairs_in"], 16 * (t + 1))
                    if later(t, 1):
                        pe.wait_ge(s["tanh_done"], t)
                    for c in range(2):
                        for tile, at in enumerate((0, CUT)):
                            o = (2 * c + tile) * 128
                            last = pe.transpose(tok_bank[:, o:o + 128], pairs[:, odd, c, at:at + 128], eye_s[:])
                    last.then_inc(s["xT_psum"], 1)
                queries(0)
                if on(a):
                    pe.wait_ge(s["score_done"], a + 1)
                    if later(a, 1):
                        pe.wait_ge(s["h_copied"], a)
                    mm(pool_bank[0:P, 0:2], eye_s[:, 0:P], score[:, par, :])
                    mm(pool_bank[0:P, 2:4], shift_s[:, 0:P], score[:, par, :]).then_inc(s["win_psum"], 1)
                token_layer(0)
                max_scores(0)
                scores(0)
                queries(1)
                token_layer(1)
                scores(1)
                if on(l):
                    pe.wait_ge(s["z2_done"], l + 1)
                    pe.wait_ge(s["att_done"], l + 1)
                    norm_transposes(turn16, z2, par).then_inc(s["z2T_psum"], 1)
                weighted(0)
                max_scores(1)
                if on(z):
                    pe.wait_ge(s["z1_done"], z + 1)
                    if on(j - 1):
                        pe.wait_ge(s["maxT_copied"], j)
                    elif later(z, 1):
                        pe.wait_ge(s["lat_lo"], z)
                    norm_transposes(lat16, z1, odd).then_inc(s["z1T_psum"], 1)
                queries(2)
                scores(2)
                if on(l):
                    pe.wait_ge(s["z2T_copied"], l + 1)
                    split_product(turn_bank[0:P, 0:E], lambda tile, lo: z2T[:, l, tile, :],
                                  lambda tile, lo: (gate_lo if lo else gate_hi)[:, tile, :]
                                  ).then_inc(s["logit_psum"], 1)
                weighted(1)
                if on(z):
                    if it_first(it, 3):
                        pe.wait_ge(s["attn_ready"], 1)
                    pe.wait_ge(s["z1T_copied"], z + 1)
                    split_product(lat_bank[:, 0:P], lambda tile, lo: (attn_lo if lo else attn_hi)[:, tile, 0:128],
                                  lambda tile, lo: z1T[:, odd, tile, :]).then_inc(s["lat_psum"], 1)
                max_scores(2)
                weighted(2)
                if on(a):
                    pe.wait_ge(s["pooled_done"], a + 1)
                    pe.wait_ge(s["win_d_done"], a + 1)
                    for tile, at in enumerate((0, CUT)):
                        last = pe.transpose(pool_bank[:, tile * P:(tile + 1) * P], pooled[:, par, at:at + 128],
                                            eye_s[0:P, 0:P])
                    last.then_inc(s["pooledT_psum"], 1)
                if on(k):
                    pe.wait_ge(s["ctxT_copied"], k + 1)
                    if on(l):
                        pe.wait_ge(s["logits_copied"], l + 1)
                    for u in range(NU):
                        last = pe.transpose(turn_bank[0:P, u * 128:(u + 1) * 128], ctxT[:, odd, u * P:(u + 1) * P],
                                            eye_s[:])
                    last.then_inc(s["att_psum"], 1)
                if on(z):
                    if on(j):
                        pe.wait_ge(s["max_done"], NU * (j + 1))
                    split_product(max_bank[0:P, 0:D], lambda tile, lo: z1T[:, odd, tile, :],
                                  lambda tile, lo: (attn_lo if lo else attn_hi)[:, tile, 128:AW]
                                  ).then_inc(s["val_psum"], 1)
                if on(j):
                    pe.wait_ge(s["max_hl_done"], j + 1)
                    if on(z):
                        pe.wait_ge(s["lat_lo"], z + 1)
                    else:
                        pe.wait_ge(s["maxT_copied"], j)
                    pe.transpose(lat16[0:2 * NH, 0:P], max_hl[:, par, :], eye16[0:P, 0:P]).then_inc(s["maxT_psum"], 1)
                if on(a):
                    pe.wait_ge(s["pooledT_copied"], a + 1)
                    for tile in range(2):
                        last = mm(pool_bank[0:P, 0:D], pooledT[:, par, tile * P:(tile + 1) * P], p_tok_s[:, tile, :],
                                  start=(tile == 0), stop=(tile == 1))
                    last.then_inc(s["h_psum"], 1)
            walk(pe, step)

            for name, count in (("tanh_done", B), ("h_copied", B), ("val_done", B), ("logits_copied", B),
                                ("q_lo", NU * B), ("max_done", NU * B), ("exp_done", NU * B), ("ctxT_copied", B),
                                ("ffn_ready", 3)):
                pe.wait_ge(s[name], count)

            def up(n, g, e, half_):
                z = z2T[:, bass.ts(g, TB), :, :]
                cols = slice(e * I, (e + 1) * I)
                for first, hi, lo, read, done in ((0, w1_hi, w1_lo, "silu_done", "h1_psum"),
                                                  (2, w3_hi, w3_lo, "inner_done", "h3_psum")):
                    if not isinstance(n, int) or n >= 2:
                        pe.wait_ge(s[read], n - 1)
                    split_product(banks[first + half_][:, 0:TB * P],
                                  lambda tile, low: (lo if low else hi)[:, tile, cols],
                                  lambda tile, low: z[:, :, tile, :]).then_inc(s[done], 1)

            def down(n, e, half_):
                pe.wait_ge(s["inner_lo_done"], n + 1)
                if not isinstance(n, int) or n >= 2:
                    pe.wait_ge(s["acc_done"], n - 1)
                for b in range(TB):
                    y = banks[4 + 2 * half_ + b // 2][0:P, (b % 2) * 256:(b % 2) * 256 + D]
                    cols = slice(b * P, (b + 1) * P)
                    mm(y, inner_hi[:, half_, cols], w2_hi[:, e, :], stop=False)
                    mm(y, inner_hi[:, half_, cols], w2_lo[:, e, :], start=False, stop=False)
                    last = mm(y, inner_lo[:, half_, cols], w2_hi[:, e, :], start=False)
                last.then_inc(s["y_psum"], 1)

            def shared_pair(q, last=False):
                up(2 * q + 1, 2 * q + 1, E, 1)
                down(2 * q, E, 0)
                up(2 * q + 2, 0 if last else 2 * q + 2, 0 if last else E, 0)
                down(2 * q + 1, E, 1)

            def experts(g, last=False):
                for e in range(E):
                    n = NG + E * g + e
                    if e < E - 1:
                        up(n + 1, g, e + 1, 1 - e % 2)
                    elif not last:
                        up(n + 1, g + 1, 0, 0)
                    down(n, e, e % 2)

            up(0, 0, E, 0)
            shared_pair(0)
            with pe.Fori(1, NG // 2 - 1) as q:
                shared_pair(q)
            shared_pair(NG // 2 - 1, last=True)
            with pe.Fori(0, NG - 1) as g:
                experts(g)
            experts(NG - 1, last=True)


def kernel(**inputs):
    import concourse.bacc as bacc
    from concourse.bass_utils import run_bass_kernel_spmd

    v = {n: np.asarray(a) for n, a in inputs.items()}
    f32 = np.float32

    def two_tiles(w, bias):
        t = np.zeros((128, 2, D), f32)
        t[:, 0] = w.T[0:128]
        t[128 - CUT:127, 1] = w.T[128:D]
        t[127, 1] = bias
        return t

    def three_tiles(w):
        t = w.T
        return np.stack([t[0:128], np.concatenate([t[128:D], t[0:R]]), t[R:D]], 1)

    last_row = np.zeros((32, D), f32)
    last_row[31] = v["L0_tok_b"]
    basis = three_tiles(v["L0_attn_basis_w"])
    heads = v["L0_attn_head_residual"].transpose(1, 0, 2)
    w1 = np.concatenate([v["L0_ffn_w1"].reshape(E * I, D), v["L0_ffn_sw1"]])
    w3 = np.concatenate([v["L0_ffn_w3"].reshape(E * I, D), v["L0_ffn_sw3"]])
    w2 = np.concatenate([v["L0_ffn_w2"], v["L0_ffn_sw2"][None]])
    shift = np.zeros((128, 128), f32)
    shift[np.arange(1, 128), np.arange(0, 127)] = 1.0
    laid = {
        "x": v["x"],
        "w_tok": two_tiles(v["L0_tok_W_w"], v["L0_tok_W_b"]),
        "b_tok": last_row,
        "v_tok": np.broadcast_to(v["L0_tok_V_w"], (128, D)),
        "vb_tok": np.broadcast_to(v["L0_tok_V_b"], (128, 1)),
        "p_tok": two_tiles(v["L0_tok_P_w"], v["L0_tok_P_b"]),
        "attn_w": np.concatenate([basis, basis, three_tiles(v["L0_attn_value_w"])], 2),
        "attn_vb": np.broadcast_to(v["L0_attn_value_b"], (128, D)),
        "core": np.tile(v["L0_attn_core"], (2, 2)),
        "head_res": np.tile(heads, (2, 1, 2)),
        "gate_w": three_tiles(v["L0_ffn_gate_weight"]),
        "gate_b": np.broadcast_to(v["L0_ffn_gate_bias"], (128, E)),
        "w1": three_tiles(w1).reshape(128, 3 * NE * I),
        "w3": three_tiles(w3).reshape(128, 3 * NE * I),
        "w2": w2.transpose(2, 0, 1),
        "eye": np.eye(128, dtype=f32),
        "shift": shift,
    }
    nc = bacc.Bacc("TRN2", target_bir_lowering=False, num_devices=1)
    arrays, args = {}, []
    for name, a in laid.items():
        a = np.ascontiguousarray(a)
        arrays[f"in_{name}"] = a
        args.append(nc.dram_tensor(f"in_{name}", a.shape, mybir.dt.from_np(a.dtype), kind="ExternalInput").ap())
    args.append(nc.dram_tensor("out", (B, P, D), F32, kind="ExternalOutput").ap())
    audio_tower(nc, *args)
    result = run_bass_kernel_spmd(nc, [arrays], core_ids=[0])
    return result.results[0]["out"]
```

```python
import numpy as np
import concourse.bass as bass
from concourse import mybir
from contextlib import ExitStack

F32 = mybir.dt.float32
F16 = mybir.dt.float16
I32 = mybir.dt.int32
ALU = mybir.AluOpType
ACT = mybir.ActivationFunctionType
AX = mybir.AxisListType

B, S, D = 64, 256, 192
PL, STRIDE = 4, 2
P = (S - PL) // STRIDE + 1
NH, R = 12, 64
HD = D // NH
HV = HD + 1
U = 4
NU = NH // U
UW = U * P
E, TOPK, G = 8, 2, 4
I = 128
NE = E + 1
CUT = D + 1 - 128
SHIFT = 2.0 ** 15
TB = 4
NG = B // TB
LAST = B + 7
HEAD, TAIL = 12, B
UNROLL = 4

HEADS_MADE, ATTN_SPLIT, HEADS_SPLIT = 0, 2, 3
W1_MAX, W3_MAX, W2_MAX, FFN_MAX, FFN_SCALES = 1, 2, 3, 4, 5
HI_SPLITS = {6: ("w2",), 7: (("w1", 0),), 8: (("w1", 1), ("w1", 2)), 9: (("w3", 0),),
             10: (("w3", 1),), 11: (("w3", 2),)}
LO_SPLITS = {7: "w2", 8: ("w1", 0), 9: ("w1", 1), 10: ("w3", 0), 11: ("w3", 1)}


def on(n):
    return not isinstance(n, int) or 0 <= n < B


def later(n, k):
    return not isinstance(n, int) or n >= k


def is_number(it, which):
    return isinstance(it, int) and it == which


def walk(eng, step):
    for it in range(HEAD):
        step(it, it % 2)
    with eng.Fori(HEAD // UNROLL, TAIL // UNROLL) as turn:
        for m in range(UNROLL):
            step(UNROLL * turn + m, m % 2)
    for it in range(TAIL, LAST):
        step(it, it % 2)


def windows(x):
    return bass.AP(tensor=x.tensor, offset=0, ap=[[S * D, B], [STRIDE * D, P], [1, PL * D]])


def audio_tower(nc, x, w_tok, b_tok, v_tok, vb_tok, p_tok, attn_w, attn_vb, core, head_res,
                gate_w, gate_b, w1, w3, w2, eye, out):
    with ExitStack() as ctx:
        def sb(name, shape, dt=F32):
            return ctx.enter_context(nc.sbuf_tensor(name, shape, dt))

        def bank(name, n=1):
            return ctx.enter_context(nc.psum_tensor(name, [128, n * 512], F32))

        def sem(name):
            return ctx.enter_context(nc.semaphore(name))

        w_tok_s = sb("w_tok_s", [128, 2, D])
        v_tok_s = sb("v_tok_s", [128, D])
        vb_s = sb("vb_s", [128, 1])
        p_tok_s = sb("p_tok_s", [128, 2, D])
        value_b = sb("value_b", [128, D])
        gate_bias = sb("gate_bias", [128, E])
        eye_s = sb("eye_s", [128, 128])
        eye16 = sb("eye16", [128, 128], F16)
        AW = 128 + D
        attn_hi = sb("attn_hi", [128, 3, AW], F16)
        attn_lo = sb("attn_lo", [128, 2, AW], F16)
        gate_hl = sb("gate_hl", [128, 3, 2, E], F16)
        w1_hi = sb("w1_hi", [128, 3, NE * I], F16)
        w1_lo = sb("w1_lo", [128, 2, NE * I], F16)
        w3_hi = sb("w3_hi", [128, 3, NE * I], F16)
        w3_lo = sb("w3_lo", [128, 2, NE * I], F16)
        w2_hi = sb("w2_hi", [128, NE, D], F16)
        w2_lo = sb("w2_lo", [128, NE, D], F16)
        head_hi = sb("head_hi", [128, NH, 128], F16)
        head_lo = sb("head_lo", [128, NH, 128], F16)
        stage = sb("stage", [128, 64 * 53])
        gate_raw = sb("gate_raw", [128, 3, E])
        head_raw = stage[:, 0:NH * 128].rearrange("p (h s) -> p h s", h=NH)
        core_raw = stage[:, NH * 128:NH * 128 + 128]
        b_tok_s = stage[:, NH * 128 + 256:NH * 128 + 256 + D]
        head_sum = stage[:, NH * 128 + 128:NH * 128 + 256]
        NSC = 7
        BASIS, VALUE, GATE, HEADS, W1, W3, W2 = range(NSC)
        amax = sb("amax", [128, NSC])
        amax_all = sb("amax_all", [128, NSC])
        power = sb("power", [128, NSC])
        inverse = sb("inverse", [128, NSC])
        exp_scale = sb("exp_scale", [128, 1])
        gate_scale = sb("gate_scale", [128, 1])
        inner_scale = sb("inner_scale", [128, 1])
        down_scale = sb("down_scale", [128, 1])
        eps = sb("eps", [128, 1])
        minus_half = sb("minus_half", [128, 1])
        zero = sb("zero", [128, 1])
        unshift = sb("unshift", [128, 1])

        pairs = sb("pairs", [128, 2, 2, D + 1])
        wins = sb("wins", [P, 2, PL, D])
        xT = sb("xT", [128, 2, 4 * 128])
        th = sb("th", [128, 2, 2 * D])
        score = sb("score", [128, 2, PL])
        win_max = sb("win_max", [P, 1])
        win_d = sb("win_d", [P, PL])
        win_e = sb("win_e", [P, PL])
        win_z = sb("win_z", [P, 1])
        win_r = sb("win_r", [P, 1])
        win_w = sb("win_w", [P, 2, PL])
        half = sb("half", [P, 2, D])
        pooled = sb("pooled", [P, 2, D + 1])
        pooledT = sb("pooledT", [128, 2, 2 * P])
        res = sb("res", [P, B, D])
        stats = sb("stats", [P, 2, 6])
        mv = sb("mv", [P, 2, 2])
        after_stats = sb("after_stats", [P, 4])
        rstd = sb("rstd", [P, 2, 1])
        vpe = sb("vpe", [P, 2, 1])
        xn = sb("xn", [P, 2, D])
        z1 = sb("z1", [P, 2, 2 * D], F16)
        z2 = sb("z2", [P, 2, 2 * D], F16)
        z1T = sb("z1T", [128, 2, 3, P], F16)
        z2T_flat = sb("z2T", [128, B * 3 * P], F16)
        z2T = z2T_flat[:].rearrange("p (b c n) -> p b c n", b=B, c=3)
        lat_a = sb("lat_a", [128, 2, P], F16)
        lat_b = sb("lat_b", [128, 2, P], F16)
        vals = sb("vals", [P, 2, NH, HV])
        q_a = sb("q_a", [128, 2, NH * P], F16)
        attn_raw = q_a[:].rearrange("p a n -> p (a n)").bitcast(F32)[:, 0:3 * AW].rearrange("p (a n) -> p a n", a=3)
        q_b = sb("q_b", [128, 2, NH * P], F16)
        row_max = sb("row_max", [P, 2, NH])
        neg_max = sb("neg_max", [P, NH])
        max_hl = sb("max_hl", [P, 2, 2 * NH], F16)
        max_hlT = sb("max_hlT", [2 * NH, 2, P], F16)
        probs = sb("probs", [P, 2, UW])
        ctxT = sb("ctxT", [128, 2, NU * P])
        recip = sb("recip", [P, NH])
        att = sb("att", [P, 2, D])
        logits = sb("logits", [P, B, E])
        late = z2T_flat[:].bitcast(F32)
        FW = 3 * NE * I
        end = B * 3 * P // 2
        w1_raw, w3_raw = (late[:, end - m * FW:end - (m - 1) * FW].rearrange("p (a n) -> p a n", a=3) for m in (1, 2))
        w2_raw = late[:, end - 2 * FW - NE * D:end - 2 * FW].rearrange("p (e d) -> p e d", e=NE)
        ffn = {"w1": (W1, w1_raw, w1_hi, w1_lo), "w3": (W3, w3_raw, w3_hi, w3_lo)}
        choice = logits
        GW = TB * P
        over_a, over_b = (q[:].rearrange("p a n -> p (a n)") for q in (q_a, q_b))
        silu = over_a[:, 0:4 * GW].bitcast(F32).rearrange("p (a n) -> p a n", a=2)
        inner = over_b[:, 0:4 * GW].bitcast(F32).rearrange("p (a n) -> p a n", a=2)
        inner_hi = over_a[:, 4 * GW:6 * GW].rearrange("p (a n) -> p a n", a=2)
        inner_lo = over_b[:, 4 * GW:6 * GW].rearrange("p (a n) -> p a n", a=2)

        sizes = (("sig", E), ("biased", E), ("masked", E), ("rank", E), ("cmp", E),
                 ("group", G), ("group_rank", G), ("group_cmp", G), ("norm", 1))
        room, at = {}, 0
        for name, width in sizes:
            room[name] = stage[0:P, at:at + B * width].rearrange("p (b e) -> p b e", e=width)
            at += B * width
        sig, biased, masked, rank, comp = (room[n] for n in ("sig", "biased", "masked", "rank", "cmp"))
        group, group_rank, group_cmp, norm = (room[n] for n in ("group", "group_rank", "group_cmp", "norm"))

        tok_bank, pool_bank, lat_bank, turn_bank = (bank(n) for n in ("tok_b", "pool_b", "lat_b_", "turn_b"))
        q_bank, max_bank, s_bank, ctx_bank = (bank(n) for n in ("q_bank", "max_b", "s_bank", "ctx_b"))
        banks = [tok_bank, pool_bank, lat_bank, turn_bank, q_bank, max_bank, s_bank, ctx_bank]
        att_ps = turn_bank[0:P, 0:NU * 128].rearrange("p (h d) -> p h d", d=32)
        lat16 = lat_bank[:, :].bitcast(F16)
        turn16 = turn_bank[:, :].bitcast(F16)

        s = {n: sem(n) for n in (
            "tok_params", "attn_params", "head_params", "w1_params", "w3_params", "w2_params",
            "amax_part", "amax_done", "prep", "consts", "tok_ready", "attn_ready", "heads_ready", "ffn_scaled",
            "ffn_hi", "ffn_lo",
            "pairs_in", "wins_in", "max_rows_in", "shifted_in",
            "xT_psum", "tok_psum", "pooledT_psum", "h_psum", "z1T_psum", "lat_psum",
            "val_psum", "q_psum", "max_psum", "s_psum", "ctx_psum", "maxT_psum", "att_psum",
            "z2T_psum", "logit_psum",
            "xT_copied", "tanh_done", "win_exp", "pooledT_copied", "h_copied", "lat_hi", "q_hi",
            "exp_done", "ctxT_copied", "z2T_copied",
            "score_part", "score_done", "win_max_done", "win_d_done", "win_z_done", "win_r_done",
            "win_w_done", "stats1", "mv1", "xn1", "stats2", "mv2", "xn2", "z1T_copied", "lat_lo",
            "val_done", "q_lo", "max_done", "maxT_copied", "recip_done", "att_done", "logits_copied",
            "vpe1", "rstd1", "z1_hi", "z1_done", "vpe2", "rstd2", "z2_hi", "z2_done", "lat_b_done",
            "prod_done", "half_done", "pooled_done", "neg_done", "max_hi", "max_hl_done", "res_done",
            "gate_tanh", "gate_step", "ranks_started", "h1_psum", "h3_psum", "silu_done", "inner_done",
            "inner_hi_done", "inner_lo_done", "y_psum", "acc_done", "stored",
        )}

        block = ctx.enter_context(nc.Block())

        @block.sync
        def _(sp):
            for dst, src in ((w_tok_s[:], w_tok), (b_tok_s[96:128, :], b_tok), (v_tok_s[:], v_tok),
                             (vb_s[:], vb_tok), (p_tok_s[:], p_tok), (eye_s[:], eye)):
                sp.dma_start(dst, src).then_inc(s["tok_params"], 16)
            for dst, src in ((attn_raw, attn_w), (value_b[:], attn_vb), (gate_raw[:], gate_w),
                             (gate_bias[:], gate_b)):
                sp.dma_start(dst, src).then_inc(s["attn_params"], 16)
            sp.dma_start(head_raw, head_res).then_inc(s["head_params"], 16)
            sp.dma_start(core_raw, core).then_inc(s["head_params"], 16)

            def step(it, par):
                n, w, a, j = it, it - 1, it - 1, it - 5
                if on(n):
                    if later(n, 1):
                        sp.wait_ge(s["xT_psum"], n)
                    sp.dma_start(pairs[:, par, :, 0:D],
                                 x[n, :, :].rearrange("(q c) d -> q c d", c=2)).then_inc(s["pairs_in"], 16)
                if on(j):
                    sp.wait_ge(s["maxT_copied"], j + 1)
                    sp.dma_start(q_b[R:R + 2, 1 - par, :].rearrange("r (h n) -> r h n", h=NH),
                                 max_hlT[:, 1 - par, :]).then_inc(s["max_rows_in"], 16)
                if on(a):
                    if later(a, 1):
                        sp.wait_ge(s["win_max_done"], a)
                    sp.wait_ge(s["score_done"], a + 1)
                    sp.dma_start(score[0:P, 1 - par, 2:4], score[1:128, 1 - par, 0:2]).then_inc(s["shifted_in"], 16)
                if on(w):
                    if later(w, 1):
                        sp.wait_ge(s["half_done"], w)
                    sp.dma_start(wins[:, 1 - par, :, :].rearrange("p l d -> p (l d)"),
                                 windows(x)[w, :, :]).then_inc(s["wins_in"], 16)
                if is_number(it, W1_MAX - 1):
                    sp.dma_start(w1_raw, w1.rearrange("p (a n) -> p a n", a=3)).then_inc(s["w1_params"], 16)
                if is_number(it, W3_MAX - 1):
                    sp.dma_start(w3_raw, w3.rearrange("p (a n) -> p a n", a=3)).then_inc(s["w3_params"], 16)
                if is_number(it, W2_MAX - 1):
                    sp.dma_start(w2_raw, w2).then_inc(s["w2_params"], 16)

            walk(sp, step)
            with sp.Fori(0, NG) as g:
                sp.wait_ge(s["acc_done"], E * (g + 1) + NG)
                sp.dma_start(out[bass.ts(g, TB), :, :].rearrange("b p d -> p b d"),
                             res[:, bass.ts(g, TB), :]).then_inc(s["stored"], 16)
            sp.wait_ge(s["stored"], 16 * NG)

        @block.gpsimd
        def _(pool):
            for m, (place, value) in enumerate((
                    (pairs[:, :, :, D:D + 1], 1.0), (pooled[:, :, D:D + 1], 1.0), (vals[:, :, :, HD:HV], 1.0),
                    (q_b[R:128, :, :], 0.0), (lat_b[R:128, :, :], 0.0), (lat_b[R:R + 2, :, :], SHIFT),
                    (eps[:], 1e-5), (minus_half[:], -0.5), (zero[:], 0.0), (unshift[:], -1.0 / SHIFT))):
                pool.memset(place, value).then_inc(s["consts"], 1)
                pool.wait_ge(s["consts"], m + 1)
            pool.wait_ge(s["amax_part"], 1)
            pool.partition_all_reduce(amax_all[:, 0:4], amax[:, 0:4], 128,
                                      bass.bass_isa.ReduceOp.absmax).then_inc(s["amax_done"], 1)

            def norm_scale(n, k, mv_done, vpe_done, rstd_done):
                pool.wait_ge(mv_done, n + 1)
                pool.tensor_tensor(vpe[:, k, :], mv[:, k, 1:2], eps[0:P, :], ALU.add).then_inc(vpe_done, 1)
                pool.wait_ge(vpe_done, n + 1)
                pool.tensor_tensor(rstd[:, k, :], vpe[:, k, :], minus_half[0:P, :],
                                   ALU.pow).then_inc(rstd_done, 1)

            def norm_lo(n, k, par, z, hi_done, lo_done):
                pool.wait_ge(hi_done, n + 1)
                pool.tensor_tensor(z[:, par, D:2 * D], xn[:, k, :], z[:, par, 0:D],
                                   ALU.subtract).then_inc(lo_done, 1)

            def step(it, par):
                n1, n2, n3, n4, n5, n6, n7, n8 = (it - back for back in range(1, 9))
                odd = 1 - par
                if on(n3):
                    norm_scale(n3, 0, s["mv1"], s["vpe1"], s["rstd1"])
                if on(n2):
                    pool.wait_ge(s["win_w_done"], n2 + 1)
                    pool.wait_ge(s["wins_in"], 16 * (n2 + 1))
                    pool.tensor_tensor(wins[:, par, :, :], wins[:, par, :, :],
                                       win_w[:, par, :].unsqueeze(2).to_broadcast([P, PL, D]),
                                       ALU.mult).then_inc(s["prod_done"], 1)
                    pool.wait_ge(s["prod_done"], n2 + 1)
                    if later(n2, 1):
                        pool.wait_ge(s["pooled_done"], n2)
                    pool.tensor_tensor(half[:], wins[:, par, 0:2, :], wins[:, par, 2:4, :],
                                       ALU.add).then_inc(s["half_done"], 1)
                if on(n3):
                    norm_lo(n3, 0, odd, z1, s["z1_hi"], s["z1_done"])
                if on(n2):
                    pool.wait_ge(s["half_done"], n2 + 1)
                    if later(n2, 2):
                        pool.wait_ge(s["pooledT_psum"], n2 - 1)
                    pool.tensor_tensor(pooled[:, par, 0:D], half[:, 0, :], half[:, 1, :],
                                       ALU.add).then_inc(s["pooled_done"], 1)
                if on(n6):
                    pool.wait_ge(s["att_done"], n6 + 1)
                    pool.tensor_tensor(res[:, n6, :], res[:, n6, :], att[:, par, :],
                                       ALU.add).then_inc(s["res_done"], 1)
                if on(n6):
                    norm_scale(n6, 1, s["mv2"], s["vpe2"], s["rstd2"])
                if on(n4):
                    pool.wait_ge(s["max_done"], NU * (n4 + 1))
                    pool.tensor_tensor(neg_max[:], row_max[:, par, :], unshift[0:P, :].to_broadcast([P, NH]),
                                       ALU.mult).then_inc(s["neg_done"], 1)
                    pool.wait_ge(s["neg_done"], n4 + 1)
                    if later(n4, 2):
                        pool.wait_ge(s["maxT_psum"], n4 - 1)
                    pool.tensor_tensor(max_hl[:, par, 0:NH], neg_max[:], zero[0:P, :].to_broadcast([P, NH]),
                                       ALU.add).then_inc(s["max_hi"], 1)
                    pool.wait_ge(s["max_hi"], n4 + 1)
                    pool.tensor_tensor(max_hl[:, par, NH:2 * NH], neg_max[:], max_hl[:, par, 0:NH],
                                       ALU.subtract).then_inc(s["max_hl_done"], 1)
                if on(n6):
                    norm_lo(n6, 1, par, z2, s["z2_hi"], s["z2_done"])
                if is_number(it, FFN_MAX):
                    pool.wait_ge(s["amax_part"], 4)
                    pool.partition_all_reduce(amax_all[:, W1:NSC], amax[:, W1:NSC], 128,
                                              bass.bass_isa.ReduceOp.absmax).then_inc(s["amax_done"], 1)

            walk(pool, step)

            started = 0
            for ranks, n in ((group_rank, G), (rank, E)):
                for e in range(n):
                    pool.memset(ranks[:, :, e:e + 1], float(n - 1 - e)).then_inc(s["ranks_started"], 1)
                    started += 1
                    pool.wait_ge(s["ranks_started"], started)

            def inner_los(n, half_):
                pool.wait_ge(s["inner_hi_done"], n + 1)
                if not isinstance(n, int) or n >= 2:
                    pool.wait_ge(s["y_psum"], n - 1)
                pool.tensor_tensor(inner_lo[:, half_, :], inner[:, half_, :], inner_hi[:, half_, :],
                                   ALU.subtract).then_inc(s["inner_lo_done"], 1)

            for m in range(2):
                inner_los(m, m)
            with pool.Fori(1, NE * NG // 2) as q:
                for m in range(2):
                    inner_los(2 * q + m, m)

        @block.scalar
        def _(act):
            def step(it, par):
                n1, n2, n3, n4, n5, n6, n7, n8 = (it - back for back in range(1, 9))
                odd = 1 - par

                def query_hi(u, n, side):
                    if not on(n):
                        return
                    act.wait_ge(s["q_psum"], NU * n + u + 1)
                    act.activation(q_a[:, side, u * UW:(u + 1) * UW], q_bank[:, 0:UW],
                                   ACT.Copy).then_inc(s["q_hi"], 1)

                def norm_hi(n, k, half_, z, xn_done, hi_done, readers):
                    act.wait_ge(xn_done, n + 1)
                    if later(n, 2):
                        act.wait_ge(readers, n - 1)
                    act.activation(z[:, half_, 0:D], xn[:, k, :], ACT.Copy).then_inc(hi_done, 1)

                def exps(u, n, side):
                    if not on(n):
                        return
                    if u == 0 and is_number(n, 0):
                        act.wait_ge(s["heads_ready"], 1)
                    act.wait_ge(s["s_psum"], NU * n + u + 1)
                    if later(n, 1) or u >= 2:
                        act.wait_ge(s["ctx_psum"], NU * n + u - 1)
                    act.activation(probs[:, (side + u) % 2, :], s_bank[0:P, 0:UW], ACT.Exp,
                                   scale=exp_scale[0:P, :]).then_inc(s["exp_done"], 1)

                query_hi(2, n5, odd)
                exps(1, n6, par)
                if on(n3):
                    act.wait_ge(s["pooledT_psum"], n3 + 1)
                    if later(n3, 2):
                        act.wait_ge(s["h_psum"], n3 - 1)
                    act.activation(pooledT[:, odd, :], pool_bank[:, 0:2 * P],
                                   ACT.Copy).then_inc(s["pooledT_copied"], 1)
                if on(n1):
                    act.wait_ge(s["xT_psum"], n1 + 1)
                    if later(n1, 2):
                        act.wait_ge(s["tok_psum"], n1 - 1)
                    act.activation(xT[:, odd, :], tok_bank[:, :], ACT.Copy).then_inc(s["xT_copied"], 1)
                if on(n4):
                    act.wait_ge(s["lat_psum"], n4 + 1)
                    if later(n4, 2):
                        act.wait_ge(s["s_psum"], NU * (n4 - 1))
                    act.activation(lat_a[:, par, :], lat_bank[:, 0:P], ACT.Copy).then_inc(s["lat_hi"], 1)
                    act.activation(lat_b[0:R, par, :], lat_bank[0:R, 0:P], ACT.Copy).then_inc(s["lat_b_done"], 1)
                exps(2, n6, par)
                if on(n3):
                    act.wait_ge(s["h_psum"], n3 + 1)
                    act.activation(res[:, n3, :], pool_bank[0:P, 0:D], ACT.Copy).then_inc(s["h_copied"], 1)
                if on(n7):
                    norm_hi(n7, 1, odd, z2, s["xn2"], s["z2_hi"], s["z2T_psum"])
                if on(n2):
                    act.wait_ge(s["win_d_done"], n2 + 1)
                    act.activation(win_e[:], win_d[:], ACT.Exp).then_inc(s["win_exp"], 1)
                if on(n5):
                    act.wait_ge(s["maxT_psum"], n5 + 1)
                    if later(n5, 2):
                        act.wait_ge(s["max_rows_in"], 16 * (n5 - 1))
                    act.activation(max_hlT[:, odd, :], lat16[0:2 * NH, 0:P], ACT.Copy).then_inc(s["maxT_copied"], 1)
                query_hi(0, n4, par)
                if on(n6):
                    act.wait_ge(s["ctx_psum"], NU * (n6 + 1))
                    if later(n6, 2):
                        act.wait_ge(s["att_psum"], n6 - 1)
                    act.activation(ctxT[:, par, :], ctx_bank[:, 0:NU * P],
                                   ACT.Copy).then_inc(s["ctxT_copied"], 1)
                if on(n7):
                    act.wait_ge(s["z2T_psum"], n7 + 1)
                    act.activation(z2T[:, n7, :, :], turn16[:, 0:384].rearrange("p (c n) -> p c n", c=3)[:, :, 0:P],
                                   ACT.Copy).then_inc(s["z2T_copied"], 1)
                if on(n1):
                    act.wait_ge(s["tok_psum"], n1 + 1)
                    if later(n1, 2):
                        act.wait_ge(s["score_done"], n1 - 1)
                    act.activation(th[:, odd, :], tok_bank[:, 0:2 * D], ACT.Tanh).then_inc(s["tanh_done"], 1)
                if on(n3):
                    norm_hi(n3, 0, odd, z1, s["xn1"], s["z1_hi"], s["z1T_psum"])
                query_hi(1, n4, par)
                exps(0, n5, odd)
                if on(n3):
                    act.wait_ge(s["z1T_psum"], n3 + 1)
                    act.activation(z1T[:, odd, :, :], lat16[:, 0:384].rearrange("p (c n) -> p c n", c=3)[:, :, 0:P],
                                   ACT.Copy).then_inc(s["z1T_copied"], 1)
                for part in HI_SPLITS.get(it, ()) if isinstance(it, int) else ():
                    if part == "w2":
                        act.wait_ge(s["ffn_scaled"], 1)
                        act.activation(w2_hi[:], w2_raw, ACT.Copy,
                                       scale=inverse[:, W2:W2 + 1]).then_inc(s["ffn_hi"], 1)
                    else:
                        c, raw, hi, lo = ffn[part[0]]
                        act.activation(hi[:, part[1], :], raw[:, part[1], :], ACT.Copy,
                                       scale=inverse[:, c:c + 1]).then_inc(s["ffn_hi"], 1)

            walk(act, step)
            act.wait_ge(s["logits_copied"], B)
            act.activation(logits[:], logits[:], ACT.Tanh, scale=gate_scale[0:P, :]).then_inc(s["gate_tanh"], 1)

            def silus(n, half_):
                act.wait_ge(s["h1_psum"], n + 1)
                if not isinstance(n, int) or n >= 2:
                    act.wait_ge(s["inner_done"], n - 1)
                act.activation(silu[:, half_, :], banks[half_][:, 0:TB * P], ACT.Silu,
                               scale=power[:, W1:W1 + 1]).then_inc(s["silu_done"], 1)

            def inner_his(n, half_):
                act.wait_ge(s["inner_done"], n + 1)
                if not isinstance(n, int) or n >= 2:
                    act.wait_ge(s["y_psum"], n - 1)
                act.activation(inner_hi[:, half_, :], inner[:, half_, :], ACT.Copy).then_inc(s["inner_hi_done"], 1)

            for m in range(2):
                silus(m, m)
                inner_his(m, m)
            with act.Fori(1, NE * NG // 2) as q:
                for m in range(2):
                    silus(2 * q + m, m)
                    inner_his(2 * q + m, m)

        @block.vector
        def _(dve):
            prepared = [0]

            def link(ins):
                prepared[0] += 1
                ins.then_inc(s["prep"], 1)
                dve.wait_ge(s["prep"], prepared[0])

            def scale_of(c0, c1):
                link(dve.tensor_scalar(amax_all[:, c0:c1], amax_all[:, c0:c1], 2.0 ** -100, None, ALU.max))
                link(dve.tensor_scalar(power[:, c0:c1].bitcast(I32), amax_all[:, c0:c1].bitcast(I32),
                                       0x7F800000, None, ALU.bitwise_and))
                link(dve.reciprocal(inverse[:, c0:c1], power[:, c0:c1]))

            def split(hi, lo, raw, lo_raw, hi_part, c):
                link(dve.tensor_scalar(hi, raw, inverse[:, c:c + 1], None, ALU.mult))
                link(dve.scalar_tensor_tensor(lo, lo_raw, inverse[:, c:c + 1], hi_part, ALU.mult, ALU.subtract))

            link(dve.memset(ctx_bank[:, :], 0.0))
            dve.wait_ge(s["tok_params"], 16 * 6)
            link(dve.tensor_copy(eye16[:], eye_s[:]))
            dve.tensor_tensor(w_tok_s[96:128, 1, :], w_tok_s[96:128, 1, :], b_tok_s[96:128, :],
                              ALU.add).then_inc(s["tok_ready"], 1)

            def biggest(c, src, axis):
                return dve.tensor_reduce(amax[:, c:c + 1], src, axis, ALU.max, apply_absolute_value=True)

            def make_heads():
                dve.wait_ge(s["head_params"], 16 * 2)
                link(dve.tensor_reduce(head_sum, head_raw.rearrange("p h s -> p s h"), AX.X, ALU.add))
                link(dve.tensor_tensor(core_raw, core_raw, head_sum, ALU.subtract))
                link(dve.tensor_scalar(core_raw, core_raw, 1.0 / NH, None, ALU.mult))
                link(dve.tensor_tensor(head_raw, head_raw, core_raw.unsqueeze(1).to_broadcast([128, NH, 128]),
                                       ALU.add))
                dve.wait_ge(s["attn_params"], 16 * 4)
                link(biggest(BASIS, attn_raw[:, 0:2, 0:128], AX.XY))
                link(biggest(VALUE, attn_raw[:, 0:2, 128:AW], AX.XY))
                link(biggest(GATE, gate_raw[:, 0:2, :], AX.XY))
                biggest(HEADS, head_raw, AX.XY).then_inc(s["amax_part"], 1)

            def split_attn():
                dve.wait_ge(s["amax_done"], 1)
                scale_of(0, 4)
                split(attn_hi[:, :, 0:128], attn_lo[:, :, 0:128], attn_raw[:, :, 0:128],
                      attn_raw[:, 0:2, 0:128], attn_hi[:, 0:2, 0:128], BASIS)
                split(attn_hi[:, :, 128:AW], attn_lo[:, :, 128:AW], attn_raw[:, :, 128:AW],
                      attn_raw[:, 0:2, 128:AW], attn_hi[:, 0:2, 128:AW], VALUE)
                link(dve.memset(gate_hl[:, 2, 1, :], 0.0))
                split(gate_hl[:, :, 0, :], gate_hl[:, 0:2, 1, :], gate_raw[:], gate_raw[:, 0:2, :],
                      gate_hl[:, 0:2, 0, :], GATE)
                dve.tensor_scalar(gate_scale[:], power[:, GATE:GATE + 1], 0.5, None,
                                  ALU.mult).then_inc(s["attn_ready"], 1)

            def split_heads():
                split(head_hi[:], head_lo[:], head_raw, head_raw, head_hi[:], HEADS)
                link(dve.tensor_tensor(exp_scale[:], power[:, BASIS:BASIS + 1], power[:, BASIS:BASIS + 1], ALU.mult))
                link(dve.tensor_tensor(exp_scale[:], exp_scale[:], power[:, HEADS:HEADS + 1], ALU.mult))
                dve.tensor_scalar(exp_scale[:], exp_scale[:], R ** -0.5, None, ALU.mult).then_inc(s["heads_ready"], 1)

            def measure(c, params, raw):
                dve.wait_ge(params, 16)
                biggest(c, raw, AX.XY).then_inc(s["amax_part"], 1)

            def scale_ffn():
                dve.wait_ge(s["amax_done"], 2)
                scale_of(W1, NSC)
                link(dve.tensor_scalar(inner_scale[:], inverse[:, W1:W1 + 1], 0.25, None, ALU.mult))
                link(dve.tensor_tensor(down_scale[:], power[:, W1:W1 + 1], power[:, W3:W3 + 1], ALU.mult))
                link(dve.tensor_tensor(down_scale[:], down_scale[:], power[:, W2:W2 + 1], ALU.mult))
                dve.tensor_scalar(down_scale[:], down_scale[:], 4.0, None, ALU.mult).then_inc(s["ffn_scaled"], 1)

            def split_lo(part):
                done = [p for i in sorted(HI_SPLITS) for p in HI_SPLITS[i]].index(part) + 1
                dve.wait_ge(s["ffn_hi"], done)
                if part == "w2":
                    dve.scalar_tensor_tensor(w2_lo[:], w2_raw, inverse[:, W2:W2 + 1], w2_hi[:],
                                             ALU.mult, ALU.subtract).then_inc(s["ffn_lo"], 1)
                else:
                    (c, raw, hi, lo), tile = ffn[part[0]], part[1]
                    dve.scalar_tensor_tensor(lo[:, tile, :], raw[:, tile, :], inverse[:, c:c + 1], hi[:, tile, :],
                                             ALU.mult, ALU.subtract).then_inc(s["ffn_lo"], 1)

            def norm_stats(n, k, stats_done):
                dve.memset(after_stats[:, k:k + 1], 0.0)
                dve.bn_stats(stats[:, k, :], res[:, n, :]).then_inc(stats_done, 1)

            def norm_mean(n, k, stats_done, mv_done):
                dve.wait_ge(stats_done, n + 1)
                dve.memset(after_stats[:, 2 + k:3 + k], 0.0)
                dve.bn_aggr(mv[:, k, :], stats[:, k, :]).then_inc(mv_done, 1)

            def normed(n, k, rstd_done, xn_done, split_done):
                dve.wait_ge(rstd_done, n + 1)
                if later(n, 1):
                    dve.wait_ge(split_done, n)
                dve.tensor_scalar(xn[:, k, :], res[:, n, :], mv[:, k, 0:1], rstd[:, k, :],
                                  ALU.subtract, ALU.mult).then_inc(xn_done, 1)

            def step(it, par):
                n1, n2, n3, n4, n5, n6, n7, n8 = (it - back for back in range(1, 9))
                odd = 1 - par

                def query_lo(u, n, side):
                    if not on(n):
                        return
                    dve.wait_ge(s["q_hi"], NU * n + u + 1)
                    dve.tensor_tensor(q_b[0:R, side, u * UW:(u + 1) * UW], q_bank[0:R, 0:UW],
                                      q_a[0:R, side, u * UW:(u + 1) * UW], ALU.subtract).then_inc(s["q_lo"], 1)

                def score_token(c, n, side):
                    if not on(n):
                        return
                    if c == 0:
                        dve.wait_ge(s["tanh_done"], n + 1)
                        if later(n, 2):
                            dve.wait_ge(s["shifted_in"], 16 * (n - 1))
                    else:
                        dve.wait_ge(s["score_part"], n + 1)
                    cols = slice(c * D, (c + 1) * D)
                    dve.tensor_tensor_reduce(
                        out=th[:, side, cols], in0=th[:, side, cols], in1=v_tok_s[:], scale=1.0,
                        scalar=vb_s[:, 0:1], op0=ALU.mult, op1=ALU.add,
                        accum_out=score[:, side, c:c + 1]).then_inc(s["score_part" if c == 0 else "score_done"], 1)

                def maxima(u, n, side):
                    if not on(n):
                        return
                    dve.wait_ge(s["max_psum"], NU * n + u + 1)
                    if u == 0 and later(n, 2):
                        dve.wait_ge(s["neg_done"], n - 1)
                    dve.tensor_reduce(row_max[:, side, u * U:(u + 1) * U],
                                      max_bank[0:P, 0:UW].rearrange("p (h m) -> p h m", h=U),
                                      AX.X, ALU.max).then_inc(s["max_done"], 1)

                maxima(2, n5, odd)
                query_lo(2, n5, odd)
                if on(n4):
                    dve.wait_ge(s["lat_b_done"], n4 + 1)
                    dve.tensor_tensor(lat_a[R:128, par, :], lat_bank[R:128, 0:P], lat_a[R:128, par, :],
                                      ALU.subtract).then_inc(s["lat_lo"], 1)
                if on(n2):
                    dve.wait_ge(s["shifted_in"], 16 * (n2 + 1))
                    dve.tensor_reduce(win_max[:], score[0:P, par, :], AX.X, ALU.max).then_inc(s["win_max_done"], 1)
                if on(n7):
                    normed(n7, 1, s["rstd2"], s["xn2"], s["z2_done"])
                if on(n2):
                    dve.wait_ge(s["win_max_done"], n2 + 1)
                    dve.tensor_scalar(win_d[:], score[0:P, par, :], win_max[:], None,
                                      ALU.subtract).then_inc(s["win_d_done"], 1)
                if on(n3):
                    dve.wait_ge(s["h_copied"], n3 + 1)
                    norm_stats(n3, 0, s["stats1"])
                if on(n2):
                    dve.wait_ge(s["win_exp"], n2 + 1)
                    dve.tensor_reduce(win_z[:], win_e[:], AX.X, ALU.add).then_inc(s["win_z_done"], 1)
                if on(n3):
                    norm_mean(n3, 0, s["stats1"], s["mv1"])
                if on(n2):
                    dve.wait_ge(s["win_z_done"], n2 + 1)
                    dve.reciprocal(win_r[:], win_z[:]).then_inc(s["win_r_done"], 1)
                if on(n2):
                    dve.wait_ge(s["win_r_done"], n2 + 1)
                    if later(n2, 2):
                        dve.wait_ge(s["prod_done"], n2 - 1)
                    dve.tensor_scalar(win_w[:, par, :], win_e[:], win_r[:], None,
                                      ALU.mult).then_inc(s["win_w_done"], 1)
                if on(n4):
                    dve.wait_ge(s["val_psum"], n4 + 1)
                    if later(n4, 2):
                        dve.wait_ge(s["ctx_psum"], NU * (n4 - 1))
                    dve.scalar_tensor_tensor(
                        vals[:, par, :, 0:HD], max_bank[0:P, 0:D].rearrange("p (h d) -> p h d", d=HD),
                        power[0:P, VALUE:VALUE + 1], value_b[0:P, :].rearrange("p (h d) -> p h d", d=HD),
                        ALU.mult, ALU.add).then_inc(s["val_done"], 1)
                query_lo(0, n4, par)
                if on(n3):
                    normed(n3, 0, s["rstd1"], s["xn1"], s["z1_done"])
                maxima(0, n4, par)
                score_token(0, n1, odd)
                if on(n7):
                    dve.wait_ge(s["logit_psum"], n7 + 1)
                    dve.tensor_reduce(logits[:, n7, :], turn_bank[0:P, 0:2 * E].rearrange("p (c e) -> p e c", c=2),
                                      AX.X, ALU.add).then_inc(s["logits_copied"], 1)
                query_lo(1, n4, par)
                score_token(1, n1, odd)
                if on(n6):
                    dve.wait_ge(s["att_psum"], n6 + 1)
                    dve.reciprocal(recip[:], att_ps[:, :, HD]).then_inc(s["recip_done"], 1)
                if on(n6):
                    dve.wait_ge(s["recip_done"], n6 + 1)
                    if later(n6, 2):
                        dve.wait_ge(s["res_done"], n6 - 1)
                    dve.tensor_tensor(att[:, par, :].rearrange("p (h d) -> p h d", d=HD), att_ps[:, :, 0:HD],
                                      recip[:].unsqueeze(2).to_broadcast([P, NH, HD]),
                                      ALU.mult).then_inc(s["att_done"], 1)
                maxima(1, n4, par)
                if on(n6):
                    dve.wait_ge(s["res_done"], n6 + 1)
                    norm_stats(n6, 1, s["stats2"])
                if on(n6):
                    norm_mean(n6, 1, s["stats2"], s["mv2"])
                if is_number(it, HEADS_MADE):
                    make_heads()
                if is_number(it, ATTN_SPLIT):
                    split_attn()
                if is_number(it, HEADS_SPLIT):
                    split_heads()
                if is_number(it, W1_MAX):
                    measure(W1, s["w1_params"], w1_raw[:, 0:2, :])
                if is_number(it, W3_MAX):
                    measure(W3, s["w3_params"], w3_raw[:, 0:2, :])
                if is_number(it, W2_MAX):
                    measure(W2, s["w2_params"], w2_raw)
                if is_number(it, FFN_SCALES):
                    scale_ffn()
                if isinstance(it, int) and it in LO_SPLITS:
                    split_lo(LO_SPLITS[it])

            walk(dve, step)

            def inners(n, half_):
                dve.wait_ge(s["silu_done"], n + 1)
                dve.wait_ge(s["h3_psum"], n + 1)
                dve.scalar_tensor_tensor(inner[:, half_, :], banks[2 + half_][:, 0:GW], inner_scale[:],
                                         silu[:, half_, :], ALU.mult, ALU.mult).then_inc(s["inner_done"], 1)

            def accumulate(n, g, e, half_):
                dve.wait_ge(s["y_psum"], n + 1)
                if not isinstance(n, int) or n >= 1:
                    dve.wait_ge(s["acc_done"], n)
                for b in range(TB):
                    y = banks[4 + 2 * half_ + b // 2][0:P, (b % 2) * 256:(b % 2) * 256 + D]
                    r = res[:, TB * g + b, :]
                    weight = down_scale[0:P, :] if e == E else choice[:, TB * g + b, e:e + 1]
                    ins = dve.scalar_tensor_tensor(r, y, weight, r, ALU.mult, ALU.add)
                ins.then_inc(s["acc_done"], 1)

            steps = [0]

            def then(ins):
                steps[0] += 1
                ins.then_inc(s["gate_step"], 1)
                dve.wait_ge(s["gate_step"], steps[0])

            def compare(out_, val, tmp, n, d):
                then(dve.tensor_tensor(tmp[:, :, 0:n - d], val[:, :, 0:n - d], val[:, :, d:n], ALU.is_ge))
                then(dve.tensor_tensor(out_[:, :, d:n], out_[:, :, d:n], tmp[:, :, 0:n - d], ALU.add))
                then(dve.tensor_tensor(out_[:, :, 0:n - d], out_[:, :, 0:n - d], tmp[:, :, 0:n - d], ALU.subtract))

            def of_group(values):
                return (values.rearrange("p b g -> p (b g)").unsqueeze(2).to_broadcast([P, B * G, E // G]))

            def gate_part(m):
                pair = biased.rearrange("p b (g e) -> p b g e", e=E // G)
                in_pairs = masked.rearrange("p b (g e) -> p (b g) e", e=E // G)
                if m == 0:
                    dve.wait_ge(s["gate_tanh"], 1)
                    then(dve.tensor_scalar(sig, logits[:], 0.5, 0.5, ALU.mult, ALU.add))
                    then(dve.tensor_tensor(biased, sig, gate_bias[0:P, :].unsqueeze(1).to_broadcast([P, B, E]),
                                           ALU.add))
                elif m == 1:
                    then(dve.tensor_tensor(group, pair[:, :, :, 0], pair[:, :, :, 1], ALU.add))
                    dve.wait_ge(s["ranks_started"], G + E)
                    compare(group_rank, group, group_cmp, G, 1)
                elif m == 2:
                    compare(group_rank, group, group_cmp, G, 2)
                elif m == 3:
                    compare(group_rank, group, group_cmp, G, 3)
                elif m == 4:
                    then(dve.tensor_scalar(group_cmp, group_rank, 1.5, None, ALU.is_lt))
                    then(dve.tensor_scalar(group, group_cmp, 1e30, -1e30, ALU.mult, ALU.add))
                elif m == 5:
                    then(dve.tensor_tensor(in_pairs, biased.rearrange("p b (g e) -> p (b g) e", e=E // G),
                                           of_group(group_cmp), ALU.mult))
                    then(dve.tensor_tensor(in_pairs, in_pairs, of_group(group), ALU.add))
                elif m < 5 + E:
                    compare(rank, masked, comp, E, m - 5)
                elif m == 5 + E:
                    then(dve.scalar_tensor_tensor(masked, rank, TOPK - 0.5, sig, ALU.is_lt, ALU.mult))
                    then(dve.tensor_reduce(norm[:, :, 0], masked, AX.X, ALU.add))
                elif m == 6 + E:
                    then(dve.tensor_scalar(norm, norm, 1e-6, None, ALU.add))
                    then(dve.reciprocal(norm, norm))
                    then(dve.tensor_scalar(norm, norm, down_scale[0:P, :], None, ALU.mult))
                else:
                    then(dve.tensor_tensor(choice[:], masked, norm.to_broadcast([P, B, E]), ALU.mult))

            inners(0, 0)
            for n in range(NG):
                inners(n + 1, (n + 1) % 2)
                accumulate(n, n, E, n % 2)
                gate_part(n)

            def experts(g, last=False):
                for e in range(E):
                    n = NG + E * g + e
                    if not (last and e == E - 1):
                        inners(n + 1, 1 - e % 2)
                    accumulate(n, g, e, e % 2)

            with dve.Fori(0, NG - 1) as g:
                experts(g)
            experts(NG - 1, last=True)

        @block.tensor
        def _(pe):
            def mm(out_, lhsT, rhs, start=True, stop=True):
                return pe.matmul(out_, lhsT, rhs, start=start, stop=stop)

            def split_product(out_, left, right):
                terms = [(0, 0), (1, 0), (2, 0), (0, 1), (1, 1)]
                for m, (tile, lo) in enumerate(terms):
                    last = mm(out_, left(tile, lo), right(tile, lo), start=(m == 0), stop=(m == len(terms) - 1))
                return last

            def norm_transposes(dst16, z, par):
                for c in range(3):
                    last = pe.transpose(dst16[:, c * 128:c * 128 + P], z[:, par, c * 128:(c + 1) * 128],
                                        eye16[0:P, 0:P])
                return last

            def step(it, par):
                n1, n2, n3, n4, n5, n6, n7, n8 = (it - back for back in range(1, 9))
                odd = 1 - par

                def queries(u, n, side):
                    if not on(n):
                        return
                    if u == 0 and is_number(n, 0):
                        pe.wait_ge(s["heads_ready"], 1)
                    if u == 0:
                        pe.wait_ge(s["lat_lo"], n + 1)
                    if later(n, 1) or u:
                        pe.wait_ge(s["q_lo"], NU * n + u)
                    for h in range(U):
                        o = q_bank[:, h * P:(h + 1) * P]
                        mm(o, head_hi[:, u * U + h, :], lat_a[:, side, :], stop=False)
                        last = mm(o, head_lo[:, u * U + h, :], lat_a[:, side, :], start=False)
                    last.then_inc(s["q_psum"], 1)

                def max_scores(u, n, side):
                    if not on(n):
                        return
                    pe.wait_ge(s["q_hi"], NU * n + u + 1)
                    if u == 0:
                        pe.wait_ge(s["val_done"], n + 1)
                    else:
                        pe.wait_ge(s["max_done"], NU * n + u)
                    for h in range(U):
                        c = (u * U + h) * P
                        last = mm(max_bank[0:P, h * P:(h + 1) * P], q_a[:, side, c:c + P], lat_a[:, side, :])
                    last.then_inc(s["max_psum"], 1)

                def scores(u, n, side):
                    if not on(n):
                        return
                    if u == 0:
                        pe.wait_ge(s["max_rows_in"], 16 * (n + 1))
                        pe.wait_ge(s["lat_b_done"], n + 1)
                        pe.wait_ge(s["q_lo"], NU * (n + 1))
                    if later(n, 1) or u:
                        pe.wait_ge(s["exp_done"], NU * n + u)
                    cols = slice(u * UW, (u + 1) * UW)
                    mm(s_bank[0:P, 0:UW], lat_a[:, side, :], q_a[:, side, cols], stop=False)
                    mm(s_bank[0:P, 0:UW], lat_b[:, side, :], q_b[:, side, cols],
                       start=False).then_inc(s["s_psum"], 1)

                def token_layer(c, n, side):
                    if not on(n):
                        return
                    pe.wait_ge(s["xT_copied"], n + 1)
                    for tile in range(2):
                        o = (2 * c + tile) * 128
                        last = mm(tok_bank[:, c * D:(c + 1) * D], xT[:, side, o:o + 128], w_tok_s[:, tile, :],
                                  start=(tile == 0), stop=(tile == 1))
                    if c == 1:
                        last.then_inc(s["tok_psum"], 1)

                def weighted(u, n, side):
                    if not on(n):
                        return
                    pe.wait_ge(s["exp_done"], NU * n + u + 1)
                    if u == 0 and later(n, 1):
                        pe.wait_ge(s["ctxT_copied"], n)
                    for h in range(U):
                        last = pe.matmul(ctx_bank[32 * h:32 * h + HV, u * P:(u + 1) * P],
                                         vals[:, side, u * U + h, :], probs[:, (side + u) % 2, h * P:(h + 1) * P],
                                         start=True, stop=True, tile_position=(0, 32 * h))
                    last.then_inc(s["ctx_psum"], 1)

                if on(n1):
                    if is_number(it, 1):
                        pe.wait_ge(s["consts"], 10)
                        pe.wait_ge(s["tok_ready"], 1)
                    pe.wait_ge(s["pairs_in"], 16 * (n1 + 1))
                    if later(n1, 1):
                        pe.wait_ge(s["tanh_done"], n1)
                    for c in range(2):
                        for tile, at in enumerate((0, CUT)):
                            o = (2 * c + tile) * 128
                            last = pe.transpose(tok_bank[:, o:o + 128], pairs[:, odd, c, at:at + 128], eye_s[:])
                    last.then_inc(s["xT_psum"], 1)
                scores(0, n6, par)
                max_scores(1, n5, odd)
                if on(n7):
                    pe.wait_ge(s["ctxT_copied"], n7 + 1)
                    if on(n8):
                        pe.wait_ge(s["logits_copied"], n8 + 1)
                    for u in range(NU):
                        last = pe.transpose(turn_bank[0:P, u * 128:(u + 1) * 128], ctxT[:, odd, u * P:(u + 1) * P],
                                            eye_s[:])
                    last.then_inc(s["att_psum"], 1)
                if on(n4):
                    pe.wait_ge(s["z1_done"], n4 + 1)
                    if on(n5 - 1):
                        pe.wait_ge(s["maxT_copied"], n5)
                    elif later(n4, 1):
                        pe.wait_ge(s["lat_lo"], n4)
                    norm_transposes(lat16, z1, par).then_inc(s["z1T_psum"], 1)
                queries(2, n5, odd)
                scores(1, n6, par)
                weighted(0, n6, par)
                if on(n4):
                    if is_number(n4, 0):
                        pe.wait_ge(s["attn_ready"], 1)
                    pe.wait_ge(s["z1T_copied"], n4 + 1)
                    split_product(lat_bank[:, 0:P], lambda tile, lo: (attn_lo if lo else attn_hi)[:, tile, 0:128],
                                  lambda tile, lo: z1T[:, par, tile, :]).then_inc(s["lat_psum"], 1)
                if on(n3):
                    pe.wait_ge(s["pooled_done"], n3 + 1)
                    if later(n3, 1):
                        pe.wait_ge(s["h_copied"], n3)
                    for tile, at in enumerate((0, CUT)):
                        last = pe.transpose(pool_bank[:, tile * P:(tile + 1) * P], pooled[:, odd, at:at + 128],
                                            eye_s[0:P, 0:P])
                    last.then_inc(s["pooledT_psum"], 1)
                max_scores(2, n5, odd)
                scores(2, n6, par)
                if on(n3):
                    pe.wait_ge(s["pooledT_copied"], n3 + 1)
                    for tile in range(2):
                        last = mm(pool_bank[0:P, 0:D], pooledT[:, odd, tile * P:(tile + 1) * P], p_tok_s[:, tile, :],
                                  start=(tile == 0), stop=(tile == 1))
                    last.then_inc(s["h_psum"], 1)
                if on(n4):
                    if on(n5):
                        pe.wait_ge(s["max_done"], NU * (n5 + 1))
                    split_product(max_bank[0:P, 0:D], lambda tile, lo: z1T[:, par, tile, :],
                                  lambda tile, lo: (attn_lo if lo else attn_hi)[:, tile, 128:AW]
                                  ).then_inc(s["val_psum"], 1)
                weighted(1, n6, par)
                weighted(2, n6, par)
                if on(n5):
                    pe.wait_ge(s["max_hl_done"], n5 + 1)
                    if on(n4):
                        pe.wait_ge(s["lat_lo"], n4 + 1)
                    else:
                        pe.wait_ge(s["maxT_copied"], n5)
                    pe.transpose(lat16[0:2 * NH, 0:P], max_hl[:, odd, :], eye16[0:P, 0:P]).then_inc(s["maxT_psum"], 1)
                queries(0, n4, par)
                token_layer(0, n1, odd)
                if on(n7):
                    pe.wait_ge(s["z2_done"], n7 + 1)
                    pe.wait_ge(s["att_done"], n7 + 1)
                    norm_transposes(turn16, z2, odd).then_inc(s["z2T_psum"], 1)
                token_layer(1, n1, odd)
                max_scores(0, n4, par)
                queries(1, n4, par)
                if on(n7):
                    pe.wait_ge(s["z2T_copied"], n7 + 1)
                    for tile in range(3):
                        last = mm(turn_bank[0:P, 0:2 * E], z2T[:, n7, tile, :],
                                  gate_hl[:, tile, :, :].rearrange("p c e -> p (c e)"),
                                  start=(tile == 0), stop=(tile == 2))
                    last.then_inc(s["logit_psum"], 1)
            walk(pe, step)

            for name, count in (("tanh_done", B), ("h_copied", B), ("val_done", B), ("logits_copied", B),
                                ("q_lo", NU * B), ("max_done", NU * B), ("exp_done", NU * B), ("ctxT_copied", B),
                                ("ffn_hi", 7), ("ffn_lo", 5)):
                pe.wait_ge(s[name], count)

            def up(n, g, e, half_):
                z = z2T[:, bass.ts(g, TB), :, :]
                cols = slice(e * I, (e + 1) * I)
                for first, hi, lo, read, done in ((0, w1_hi, w1_lo, "silu_done", "h1_psum"),
                                                  (2, w3_hi, w3_lo, "inner_done", "h3_psum")):
                    if not isinstance(n, int) or n >= 2:
                        pe.wait_ge(s[read], n - 1)
                    split_product(banks[first + half_][:, 0:TB * P],
                                  lambda tile, low: (lo if low else hi)[:, tile, cols],
                                  lambda tile, low: z[:, :, tile, :]).then_inc(s[done], 1)

            def down(n, e, half_):
                pe.wait_ge(s["inner_lo_done"], n + 1)
                if not isinstance(n, int) or n >= 2:
                    pe.wait_ge(s["acc_done"], n - 1)
                for b in range(TB):
                    y = banks[4 + 2 * half_ + b // 2][0:P, (b % 2) * 256:(b % 2) * 256 + D]
                    cols = slice(b * P, (b + 1) * P)
                    mm(y, inner_hi[:, half_, cols], w2_hi[:, e, :], stop=False)
                    mm(y, inner_hi[:, half_, cols], w2_lo[:, e, :], start=False, stop=False)
                    last = mm(y, inner_lo[:, half_, cols], w2_hi[:, e, :], start=False)
                last.then_inc(s["y_psum"], 1)

            def shared_pair(q, last=False):
                up(2 * q + 1, 2 * q + 1, E, 1)
                down(2 * q, E, 0)
                up(2 * q + 2, 0 if last else 2 * q + 2, 0 if last else E, 0)
                down(2 * q + 1, E, 1)

            def experts(g, last=False):
                for e in range(E):
                    n = NG + E * g + e
                    if e < E - 1:
                        up(n + 1, g, e + 1, 1 - e % 2)
                    elif not last:
                        up(n + 1, g + 1, 0, 0)
                    down(n, e, e % 2)

            up(0, 0, E, 0)
            shared_pair(0)
            with pe.Fori(1, NG // 2 - 1) as q:
                shared_pair(q)
            shared_pair(NG // 2 - 1, last=True)
            with pe.Fori(0, NG - 1) as g:
                experts(g)
            experts(NG - 1, last=True)


def kernel(**inputs):
    import concourse.bacc as bacc
    from concourse.bass_utils import run_bass_kernel_spmd

    v = {n: np.asarray(a) for n, a in inputs.items()}
    f32 = np.float32

    def two_tiles(w, bias):
        t = np.zeros((128, 2, D), f32)
        t[:, 0] = w.T[0:128]
        t[128 - CUT:127, 1] = w.T[128:D]
        t[127, 1] = bias
        return t

    def three_tiles(w):
        t = w.T
        return np.stack([t[0:128], np.concatenate([t[128:D], t[0:R]]), t[R:D]], 1)

    last_row = np.zeros((32, D), f32)
    last_row[31] = v["L0_tok_b"]
    basis = three_tiles(v["L0_attn_basis_w"])
    heads = v["L0_attn_head_residual"].transpose(1, 0, 2)
    w1 = np.concatenate([v["L0_ffn_w1"].reshape(E * I, D), v["L0_ffn_sw1"]])
    w3 = np.concatenate([v["L0_ffn_w3"].reshape(E * I, D), v["L0_ffn_sw3"]])
    w2 = np.concatenate([v["L0_ffn_w2"], v["L0_ffn_sw2"][None]])
    laid = {
        "x": v["x"],
        "w_tok": two_tiles(v["L0_tok_W_w"], v["L0_tok_W_b"]),
        "b_tok": last_row,
        "v_tok": np.broadcast_to(v["L0_tok_V_w"], (128, D)),
        "vb_tok": np.broadcast_to(v["L0_tok_V_b"], (128, 1)),
        "p_tok": two_tiles(v["L0_tok_P_w"], v["L0_tok_P_b"]),
        "attn_w": np.concatenate([basis, basis, three_tiles(v["L0_attn_value_w"])], 2),
        "attn_vb": np.broadcast_to(v["L0_attn_value_b"], (128, D)),
        "core": np.tile(v["L0_attn_core"], (2, 2)),
        "head_res": np.tile(heads, (2, 1, 2)),
        "gate_w": three_tiles(v["L0_ffn_gate_weight"]),
        "gate_b": np.broadcast_to(v["L0_ffn_gate_bias"], (128, E)),
        "w1": three_tiles(w1).reshape(128, 3 * NE * I),
        "w3": three_tiles(w3).reshape(128, 3 * NE * I),
        "w2": w2.transpose(2, 0, 1),
        "eye": np.eye(128, dtype=f32),
    }
    nc = bacc.Bacc("TRN2", target_bir_lowering=False, num_devices=1)
    arrays, args = {}, []
    for name, a in laid.items():
        a = np.ascontiguousarray(a)
        arrays[f"in_{name}"] = a
        args.append(nc.dram_tensor(f"in_{name}", a.shape, mybir.dt.from_np(a.dtype), kind="ExternalInput").ap())
    args.append(nc.dram_tensor("out", (B, P, D), F32, kind="ExternalOutput").ap())
    audio_tower(nc, *args)
    result = run_bass_kernel_spmd(nc, [arrays], core_ids=[0])
    return result.results[0]["out"]
```
